# Optimizing a Trainium2 kernel written in Bass

```python
import numpy as np
import jax
import jax.numpy as jnp

def _softmax(x, axis=-1):
    return jax.nn.softmax(x, axis=axis)

def _gelu(x):
    return jax.nn.gelu(x, approximate=True)

def _silu(x):
    return jax.nn.silu(x)

def _sigmoid(x):
    return jax.nn.sigmoid(x)

def _layernorm(x, axis=-1, eps=1e-05):
    m = jnp.mean(x, axis=axis, keepdims=True)
    v = jnp.var(x, axis=axis, keepdims=True)
    return (x - m) / jnp.sqrt(v + eps)

def _scatter_add(tgt, idx, src, axis=0):
    return tgt.at[idx].add(src)

def _segment_sum(src, seg, n):
    return jax.ops.segment_sum(src, seg, n)
kernel_name = 'mk_sandwich_d1_jaxref_r4_6669b2'

def setup_inputs(seed: int=0):
    np.random.seed(seed)
    _w = jnp.asarray

    def _L0_attn_setup():
        import math
        import jax, jax.numpy as jnp
        import numpy as np
        B, S, D, H, DH = (2, 512, 256, 16, 64)
        INNER = H * DH

        def _l2norm(t):
            n = jnp.linalg.norm(t, axis=-1, keepdims=True)
            return t / jnp.maximum(n, 1e-12)
        key = jax.random.key(seed)
        k0, k1, k2, k3 = jax.random.split(key, 4)
        x = jax.random.normal(k0, (B, S, D), dtype=jnp.float32)
        w_q = jax.random.normal(k1, (D, INNER), dtype=jnp.float32) * 0.02
        w_kv = jax.random.normal(k2, (D, 2 * INNER), dtype=jnp.float32) * 0.02
        w_out = jax.random.normal(k3, (INNER, D), dtype=jnp.float32) * 0.02
        b_out = jnp.zeros((D,), dtype=jnp.float32)
        scale_init = -math.log(math.log2(S ** 2 - S))
        scale = jnp.full((1, H, 1, 1), scale_init, dtype=jnp.float32)
        return {'x': x, 'w_q': w_q, 'w_kv': w_kv, 'w_out': w_out, 'b_out': b_out, 'scale': scale}
    _L0_attn_in = _L0_attn_setup()

    def _L0_ffn_setup():
        import jax, jax.numpy as jnp
        import numpy as np
        D_IN, D_HID = (256, 1024)

        def _ternary(key, shape):
            return jax.random.randint(key, shape, -1, 2).astype(jnp.float32)

        def _tlin(x, w, s):
            return jnp.einsum('bsi,oi->bso', x, w) * s
        key = jax.random.key(seed)
        ks = jax.random.split(key, 12)
        inv = lambda fan: 1.0 / np.sqrt(fan).astype(np.float32)
        return {'x': jax.random.normal(ks[0], (4, 512, D_IN), dtype=jnp.float32), 'w1_w': _ternary(ks[1], (D_HID, D_IN)), 'w1_s': jax.random.uniform(ks[2], (D_HID,), dtype=jnp.float32) * inv(D_IN), 'w2_w': _ternary(ks[3], (D_HID, D_IN)), 'w2_s': jax.random.uniform(ks[4], (D_HID,), dtype=jnp.float32) * inv(D_IN), 'h1_w': _ternary(ks[5], (D_HID, D_HID)), 'h1_s': jax.random.uniform(ks[6], (D_HID,), dtype=jnp.float32) * inv(D_HID), 'h2_w': _ternary(ks[7], (D_HID, D_HID)), 'h2_s': jax.random.uniform(ks[8], (D_HID,), dtype=jnp.float32) * inv(D_HID), 'w3_w': _ternary(ks[9], (D_IN, D_HID)), 'w3_s': jax.random.uniform(ks[10], (D_IN,), dtype=jnp.float32) * inv(D_HID)}
    _L0_ffn_in = _L0_ffn_setup()
    _d = {'L0_attn_x': _L0_attn_in['x'], 'L0_attn_w_q': _L0_attn_in['w_q'], 'L0_attn_w_kv': _L0_attn_in['w_kv'], 'L0_attn_w_out': _L0_attn_in['w_out'], 'L0_attn_b_out': _L0_attn_in['b_out'], 'L0_attn_scale': _L0_attn_in['scale'], 'L0_ffn_w1_w': _L0_ffn_in['w1_w'], 'L0_ffn_w1_s': _L0_ffn_in['w1_s'], 'L0_ffn_w2_w': _L0_ffn_in['w2_w'], 'L0_ffn_w2_s': _L0_ffn_in['w2_s'], 'L0_ffn_h1_w': _L0_ffn_in['h1_w'], 'L0_ffn_h1_s': _L0_ffn_in['h1_s'], 'L0_ffn_h2_w': _L0_ffn_in['h2_w'], 'L0_ffn_h2_s': _L0_ffn_in['h2_s'], 'L0_ffn_w3_w': _L0_ffn_in['w3_w'], 'L0_ffn_w3_s': _L0_ffn_in['w3_s']}
    _x0 = _d['L0_attn_x']
    _d['L0_attn_x'] = jax.random.normal(jax.random.fold_in(jax.random.key(seed), 1), (8, 512, 256), dtype=_x0.dtype)
    del _x0
    return _d

def reference(L0_attn_x, L0_attn_w_q, L0_attn_w_kv, L0_attn_w_out, L0_attn_b_out, L0_attn_scale, L0_ffn_w1_w, L0_ffn_w1_s, L0_ffn_w2_w, L0_ffn_w2_s, L0_ffn_h1_w, L0_ffn_h1_s, L0_ffn_h2_w, L0_ffn_h2_s, L0_ffn_w3_w, L0_ffn_w3_s):

    def _L0_attn_ref(x, w_q, w_kv, w_out, b_out, scale):
        import math
        import jax, jax.numpy as jnp
        import numpy as np
        B, S, D, H, DH = (2, 512, 256, 16, 64)
        INNER = H * DH

        def _l2norm(t):
            n = jnp.linalg.norm(t, axis=-1, keepdims=True)
            return t / jnp.maximum(n, 1e-12)
        b, s, _ = x.shape
        h = scale.shape[1]
        q = (x @ w_q).reshape(b, s, h, -1).transpose(0, 2, 1, 3)
        kv = x @ w_kv
        k, v = jnp.split(kv, 2, axis=-1)
        k = k.reshape(b, s, h, -1).transpose(0, 2, 1, 3)
        v = v.reshape(b, s, h, -1).transpose(0, 2, 1, 3)
        q = _l2norm(q) * jnp.exp(scale)
        k = _l2norm(k)
        sim = jnp.einsum('bhid,bhjd->bhij', q, k)
        attn = jax.nn.softmax(sim, axis=-1)
        out = jnp.einsum('bhij,bhjd->bhid', attn, v)
        out = out.transpose(0, 2, 1, 3).reshape(b, s, h * out.shape[-1])
        return out @ w_out + b_out

    def _L0_ffn_ref(x, w1_w, w1_s, w2_w, w2_s, h1_w, h1_s, h2_w, h2_s, w3_w, w3_s):
        import jax, jax.numpy as jnp
        import numpy as np
        D_IN, D_HID = (256, 1024)

        def _ternary(key, shape):
            return jax.random.randint(key, shape, -1, 2).astype(jnp.float32)

        def _tlin(x, w, s):
            return jnp.einsum('bsi,oi->bso', x, w) * s
        h = jax.nn.silu(_tlin(x, w1_w, w1_s)) * _tlin(x, w2_w, w2_s)
        h = jax.nn.gelu(_tlin(h, h1_w, h1_s), approximate=False)
        h = jax.nn.gelu(_tlin(h, h2_w, h2_s), approximate=False)
        return _tlin(h, w3_w, w3_s)
    x = L0_attn_x
    x = x + _layernorm(_L0_attn_ref(_layernorm(x, axis=-1), L0_attn_w_q, L0_attn_w_kv, L0_attn_w_out, L0_attn_b_out, L0_attn_scale), axis=-1)
    x = x + _layernorm(_L0_ffn_ref(_layernorm(x, axis=-1), L0_ffn_w1_w, L0_ffn_w1_s, L0_ffn_w2_w, L0_ffn_w2_s, L0_ffn_h1_w, L0_ffn_h1_s, L0_ffn_h2_w, L0_ffn_h2_s, L0_ffn_w3_w, L0_ffn_w3_s), axis=-1)
    return x

_drawn_inputs = setup_inputs


def setup_inputs(seed=0):
    import zlib

    import numpy as np

    out = dict(_drawn_inputs(seed))
    spreads = {'L0_attn_b_out': (0.0, 0.1), 'L0_attn_scale': (-2.8902151584625244, 0.2)}
    factors = {}
    for name, (base, spread) in spreads.items():
        noise = np.random.default_rng([zlib.crc32(name.encode()), seed]).standard_normal(out[name].shape)
        drawn = base * np.exp(spread * noise) if base else spread * noise
        out[name] = jnp.asarray(drawn.astype(out[name].dtype))
    for name, factor in factors.items():
        out[name] = (out[name] * factor).astype(out[name].dtype)
    return out
```

```python
import concourse.bass as bass
from concourse import mybir
from contextlib import ExitStack
import numpy as np

B, S, D, H, DH = 8, 512, 256, 16, 64
HP = H // 2
NT = S // 128
HID = 1024
KH = HID // 128
EPS = 1e-5
TINY = 1e-24
TOP = 80.0


class Program:

    def __init__(self):
        self.ops = {"pe": [], "act": [], "dve": [], "pool": [], "sp": []}
        self.value = {}

    def do(self, engine, fn, after=(), inc=None, by=1):
        self.ops[engine].append((fn, [e for e in after if e is not None], inc, by))
        if inc is None:
            return None
        self.value[inc] = self.value.get(inc, 0) + by
        return (inc, self.value[inc])

    def dma(self, engine, out, in_, after=(), inc=None):
        return self.do(engine, lambda e: e.dma_start(out, in_), after, inc, 16)

    def capture(self, engine, build):
        kept, self.ops[engine] = self.ops[engine], []
        build()
        taken, self.ops[engine] = self.ops[engine], kept
        return taken

    def branch(self, engine, flag, nonzero, zero=()):
        self.ops[engine].append((flag, nonzero, zero))

    def issue(self, name, engine, sems, reached):
        self.put(self.ops[name], engine, sems, reached)
        self.ops[name] = []

    def put(self, ops, engine, sems, reached):
        for op in ops:
            if len(op) == 3:
                flag, nonzero, zero = op
                word = engine.value_load(flag)
                with engine.If(word != 0):
                    self.put(nonzero, engine, sems, dict(reached))
                if zero:
                    with engine.Else():
                        self.put(zero, engine, sems, dict(reached))
                continue
            fn, after, inc, by = op
            for sem, value in after:
                if reached.get(sem, 0) < value:
                    engine.wait_ge(sems[sem], value)
                    reached[sem] = value
            if fn is None:
                continue
            done = fn(engine)
            if inc is not None:
                done.then_inc(sems[inc], by)


def run_blocks(nc, ctx, p, sems):
    for s in sorted(p.value):
        if s not in sems:
            sems[s] = ctx.enter_context(nc.semaphore("s_" + s))
    with nc.Block() as block:
        @block.sync
        def _(e):
            p.issue("sp", e, sems, {})

        @block.gpsimd
        def _(e):
            p.issue("pool", e, sems, {})

        @block.scalar
        def _(e):
            p.issue("act", e, sems, {})

        @block.vector
        def _(e):
            p.issue("dve", e, sems, {})

        @block.tensor
        def _(e):
            p.issue("pe", e, sems, {})


def attention(nc, p, sb, pb, x, wqkv, wout, bout, scale, x1):
    f32, f32r = mybir.dt.float32, mybir.dt.float32r
    ALU, ACT, AX = mybir.AluOpType, mybir.ActivationFunctionType, mybir.AxisListType
    E = {}
    get = E.get

    wh = sb("wh", [128, 2, 4, 768], f32r)
    wl = sb("wl", [128, 2, 4, 768], f32r)
    oh = sb("oh", [128, HP, 256], f32r)
    ol = sb("ol", [128, HP, 256], f32r)
    xt = sb("xt", [128, NT, 256], f32)
    xr = sb("xr", [128, NT, 256], f32)
    xh = sb("xh", [128, 2, 512], f32r)
    xl = sb("xl", [128, 2, 512], f32r)
    qk = sb("qk", [128, 3, NT, 256], f32)
    th = sb("th", [128, 2, 2, 512], f32r)
    tl = sb("tl", [128, 2, 2, 512], f32r)
    V = sb("V", [128, 2, NT, 512], f32r)
    P = sb("P", [128, 3, 1024], f32)
    Ph = sb("Ph", [128, 3, 1024], f32r)
    Pl = sb("Pl", [128, 3, 1024], f32r)
    A = sb("A", [128, 2, 512], f32)
    ah = sb("ah", [128, 2, 512], f32r)
    al = sb("al", [128, 2, 512], f32r)
    ot = sb("ot", [128, 512], f32)
    Or = sb("Or", [128, 6, 512], f32)
    rc = sb("rc", [128, 512], f32)
    rh = sb("rh", [128, 512], f32r)
    rl = sb("rl", [128, 512], f32r)
    nh = sb("nh", [128, 512], f32r)
    nl = sb("nl", [128, 512], f32r)
    sq = sb("sq", [128, 512], f32)
    ident = sb("ident", [128, 128], f32)
    seld = sb("seld", [128, 240], f32r)
    selr = sb("selr", [128, 4, 128], f32r)
    bb = sb("bb", [128, 256], f32)
    es = sb("es", [128, H], f32)
    sh = sb("sh", [128, H], f32)
    half = sb("half", [128, 8], f32)
    ss = sb("ss", [128, 2, 8], f32)
    rs = sb("rs", [128, 2, 8], f32)
    st = sb("st", [128, NT, 6], f32)
    mv = sb("mv", [128, NT, 2], f32)
    ve = sb("ve", [128, NT], f32)
    rd = sb("rd", [128, NT], f32)
    st2 = sb("st2", [128, NT, 6], f32)
    mv2 = sb("mv2", [128, NT, 2], f32)
    ve2 = sb("ve2", [128, NT], f32)
    rd2 = sb("rd2", [128, NT], f32)

    SB = [pb(f"S{i}", [128, 512], f32) for i in range(2)]
    G = [pb(f"G{i}", [128, 512], f32) for i in range(2)]
    OB = pb("OB", [128, 512], f32)
    DB = pb("DB", [128, 512], f32)
    YB = [pb(f"Y{i}", [128, 512], f32) for i in range(2)]

    p.do("pool", lambda e: e.memset(ident[:, :], 0.0), inc="c0")
    p.do("pool", lambda e: e.memset(half[:, :], -0.5), inc="c0")
    p.do("pool", lambda e: e.memset(A[:, :, :], 0.0), inc="c0")
    c0 = p.do("pool", lambda e: e.memset(P[:, 0, 0:240], 0.0), inc="c0")
    E["ident"] = p.do("pool", lambda e: e.affine_select(
        out=ident[:, :], in_=ident[:, :], compare_op=ALU.not_equal, fill=1.0, base=0,
        pattern=[[-1, 128]], channel_multiplier=1), [c0], inc="c1")
    c2 = p.do("pool", lambda e: e.memset(P[:, 0, 112:128], 1.0), [c0], inc="c1")
    c3 = p.do("pool", lambda e: e.affine_select(
        out=A[:, 0, :].rearrange("p (b c d) -> p b c d", b=4, c=2),
        in_=A[:, 0, :].rearrange("p (b c d) -> p b c d", b=4, c=2),
        compare_op=ALU.not_equal, fill=1.0, base=0,
        pattern=[[-32, 4], [-16, 2], [0, 64]], channel_multiplier=1), [c0], inc="c1")
    E["seld"] = p.do("dve", lambda e: e.tensor_copy(seld[:, :], P[:, 0, 0:240]), [c2], inc="c2")
    E["selr"] = p.do("dve", lambda e: e.tensor_copy(
        selr[:, :, :].rearrange("p a b -> p (a b)"), A[:, 0, :]),
        [c3], inc="c2")
    E["bb"] = p.dma("act", bb[:, :], bout, inc="bb")
    ld = p.dma("act", es[:, :], scale, inc="sc")
    E["es"] = p.do("act", lambda e: e.activation(es[:, :], es[:, :], ACT.Exp), [ld], inc="es")
    sh0 = p.do("dve", lambda e: e.tensor_scalar(sh[:, :], es[:, :], -1.0, TOP, ALU.mult, ALU.add),
               [E["es"]], inc="sh")
    E["sh"] = p.do("dve", lambda e: e.tensor_scalar_min(sh[:, :], sh[:, :], 0.0), [sh0], inc="sh")

    g_at = [0]
    g_free = [[], []]

    def g_take():
        i = g_at[0] % 2
        g_at[0] += 1
        return i, g_free[i]

    def split(psum, hi, lo, after, name, free=()):
        a = p.do("act", lambda e: e.activation(hi, psum, ACT.Copy), [after, *free], inc=name + "h")
        b = p.do("dve", lambda e: e.tensor_tensor(lo, psum, hi.bitcast(f32), ALU.subtract),
                 [a, *free], inc=name + "l")
        return a, b

    stage = [P[:, i, 0:768] for i in range(3)]
    sfree = [[E["seld"]], [], []]
    n = 0
    for q in range(4):
        for k in range(2):
            i = n % 3
            ld = p.dma("sp", stage[i], wqkv[:, k, q, :], sfree[i], inc=f"wld{i}")
            a = p.do("act", lambda e, i=i, q=q, k=k: e.activation(wh[:, k, q, :], stage[i], ACT.Copy),
                     [ld], inc="wh")
            b = p.do("dve", lambda e, i=i, q=q, k=k: e.tensor_tensor(
                wl[:, k, q, :], stage[i], wh[:, k, q, :].bitcast(f32), ALU.subtract), [a], inc="wl")
            sfree[i] = [a, b]
            E["w", q] = [a, b]
            n += 1
            if n == 2:
                def late_x():
                    E["x", 0] = p.dma("sp", xt[:, :, :], x[0], inc="x")
                late_x()
    for k in range(2):
        i = n % 3
        src = P[:, i, 0:1024].rearrange("p (a b) -> p a b", a=4)
        ld = p.dma("sp", src, wout[:, 4 * k:4 * k + 4, :], sfree[i], inc=f"wld{i}")
        a = p.do("act", lambda e, s=src, k=k: e.activation(oh[:, 4 * k:4 * k + 4, :], s, ACT.Copy),
                 [ld], inc="wh")
        b = p.do("dve", lambda e, s=src, k=k: e.tensor_tensor(
            ol[:, 4 * k:4 * k + 4, :], s, oh[:, 4 * k:4 * k + 4, :].bitcast(f32), ALU.subtract),
            [a], inc="wl")
        sfree[i] = [a, b]
        n += 1
    E["wout"] = [a, b]
    for i in range(3):
        E["Pfree", i - 3] = sfree[i]

    def load_x(b):
        E["x", b] = p.dma("sp", xt[:, :, :], x[b], [get(("xT", b - 1))], inc="x")

    def stats(src, t, st, mv, ready, name):
        a = p.do("dve", lambda e: e.bn_stats(st[:, t, :], src), ready, inc=name + "a")
        return p.do("dve", lambda e: e.bn_aggr(mv[:, t, :], st[:, t, :]), [a], inc=name + "b")

    def ln1(b):
        for t in range(NT):
            m = stats(xt[:, t, :], t, st, mv, [E["x", b], get(("ln", b - 1))], "ln1")
        v = p.do("dve", lambda e: e.tensor_scalar_add(ve[:, :], mv[:, :, 1], EPS), [m], inc="ve")
        r = p.do("pool", lambda e: e.tensor_tensor(rd[:, :], ve[:, :], half[:, 0:NT], ALU.pow),
                 [v, c0], inc="rd")
        for t in range(NT):
            E["ln", b] = p.do("dve", lambda e, t=t: e.tensor_scalar(
                xt[:, t, :], xt[:, t, :], mv[:, t, 0:1], rd[:, t:t + 1], ALU.subtract, ALU.mult),
                [r], inc="xn")

    def x_turn(b, k):
        i, free = g_take()
        for t in range(NT):
            d = p.do("pe", lambda e, t=t: e.transpose(
                G[i][:, t * 128:(t + 1) * 128], xt[:, t, k * 128:(k + 1) * 128], ident[:, :]),
                [E["ln", b], E["ident"], *free] if t == 0 else (), inc="xT" if t == NT - 1 else None)
        E["xT", b] = d
        g_free[i] = split(G[i][:, :], xh[:, k, :], xl[:, k, :], d, "x", [get(("v", b - 1, 3))])
        E["xs", b] = g_free[i]

    def terms(ps, ah_, al_, bh, bl, first, last):
        todo = [(ah_, bh), (al_, bh), (ah_, bl)]
        for n_, (l, r) in enumerate(todo):
            yield (lambda e, l=l, r=r, n_=n_: e.matmul(
                ps, l, r, start=first and n_ == 0, stop=last and n_ == 2, skip_group_check=True))

    def project(b, q, t, c0_, c1_, ps, after, inc):
        fns = []
        for k in range(2):
            xs = slice(t * 128, (t + 1) * 128)
            fns += list(terms(ps, xh[:, k, xs], xl[:, k, xs], wh[:, k, q, c0_:c1_], wl[:, k, q, c0_:c1_],
                              k == 0, k == 1))
        for n_, fn in enumerate(fns):
            d = p.do("pe", fn, after if n_ == 0 else (), inc=inc if n_ == len(fns) - 1 else None)
        return d

    def qk_tile(b, q, t):
        i, free = g_take()
        d = project(b, q, t, 0, 512, G[i][:, :], [*E["xs", b], *E["w", q], *free], "qk")
        hp = b * HP + 2 * q
        u = (b * 4 + q) * NT + t
        for j in range(2):
            n_ = hp + j
            c = p.do("act", lambda e, j=j, n_=n_: e.activation(
                qk[:, n_ % 3, t, :], G[i][:, j * 256:(j + 1) * 256], ACT.Copy),
                [d, get(("T", n_ - 3))], inc="qkc")
        s = p.do("act", lambda e: e.activation(sq[:, :], G[i][:, :], ACT.Square),
                 [get(("ssum", u - 1))], inc="sq")
        g_free[i] = [s]
        m0 = p.do("dve", lambda e: e.reduce_sum(
            ss[:, u % 2, :], sq[:, :].rearrange("p (h d) -> p h d", d=DH), AX.X),
            [s, get(("rs", u - 2))], inc="ssum")
        E["ssum", u] = m0
        m1 = p.do("dve", lambda e: e.tensor_scalar_max(ss[:, u % 2, :], ss[:, u % 2, :], TINY),
                  [m0], inc="smax")
        E["rs", u] = p.do("pool", lambda e: e.tensor_tensor(
            rs[:, u % 2, :], ss[:, u % 2, :], half[:, :], ALU.pow), [m1, get(("qkn", u - 2))], inc="rs")
        return u, hp, t, c

    def qk_scale(u, hp, t, c):
        for j in range(2):
            a = qk[:, (hp + j) % 3, t, :].rearrange("p (h d) -> p h d", d=DH)
            r = rs[:, u % 2, 4 * j:4 * j + 4].unsqueeze(2).to_broadcast([128, 4, DH])
            E["qkn", u] = E["qkr", hp + j] = p.do(
                "dve", lambda e, a=a, r=r: e.tensor_tensor(a, a, r, ALU.mult), [E["rs", u], c], inc="qkn")

    def v_tiles(b, q, half_):
        i, free = g_take()
        s = (b * 4 + q) % 2
        for t in (2 * half_, 2 * half_ + 1):
            o = (t % 2) * 256
            d = project(b, q, t, 512, 768, G[i][:, o:o + 256],
                        [*E["xs", b], *free] if t % 2 == 0 else (), "v")
        prev = b * 4 + q - 2
        w = [d, get(("pv", 4 * prev + 3))]
        moves = []
        for t in (2 * half_, 2 * half_ + 1):
            o = (t % 2) * 256
            src = G[i][:, o:o + 256].rearrange("p (a b d) -> p a b d", a=2, b=2)
            vv = V[:, s, t, :].rearrange("p (a s d) -> p a s d", a=2, s=4)
            for b_ in range(2):
                moves.append((src[:, :, b_, :], vv[:, :, 3 * b_, :], vv[:, :, 1 + b_, :]))
        for src, hi, lo in moves:
            x_ = p.do("act", lambda e, src=src, hi=hi: e.activation(hi, src, ACT.Copy), w, inc="vh")
        for src, hi, lo in moves:
            y_ = p.do("dve", lambda e, src=src, hi=hi, lo=lo: e.tensor_tensor(
                lo, src, hi.bitcast(f32), ALU.subtract), [x_, *w], inc="vl")
        g_free[i] = [x_, y_]
        E["v", b, q] = d
        E["vs", b * 4 + q] = [x_, y_]

    def turn(n_):
        for j in range(2):
            i, free = g_take()
            for t in range(NT):
                d = p.do("pe", lambda e, i=i, j=j, t=t: e.transpose(
                    G[i][:, t * 128:(t + 1) * 128], qk[:, n_ % 3, t, j * 128:(j + 1) * 128], ident[:, :]),
                    [E["qkr", n_], *free] if t == 0 else (), inc="T" if t == NT - 1 else None)
            g_free[i] = split(G[i][:, :], th[:, n_ % 2, j, :], tl[:, n_ % 2, j, :], d, "t",
                              [get(("s", 2 * (n_ - 2) + 1, NT - 1))])
        E["T", n_] = d
        E["ts", n_] = g_free[i]

    def scores(g, jt):
        n_, r = g // 2, 64 * (g % 2)
        b_ = (NT * g + jt) % 2
        js = slice(jt * 128, (jt + 1) * 128)
        kh, kl = th[r:r + 64, n_ % 2, 1, js], tl[r:r + 64, n_ % 2, 1, js]
        qh, ql = th[r:r + 64, n_ % 2, 0, :], tl[r:r + 64, n_ % 2, 0, :]
        before = get(("exp", g, jt - 2)) if jt >= 2 else get(("exp", g - 1, jt + 2))
        for m, fn in enumerate(terms(SB[b_][:, :], kh, kl, qh, ql, True, True)):
            d = p.do("pe", fn, [*E["ts", n_], before] if m == 0 else (), inc="s" if m == 2 else None)
        E["s", g, jt] = d
        h = g % H
        u = 2 * g + jt // 2
        c = (jt % 2) * 512
        E["exp", g, jt] = p.do("act", lambda e: e.activation(
            P[:, u % 3, c:c + 512], SB[b_][:, :], ACT.Exp, bias=sh[:, h:h + 1], scale=es[:, h:h + 1]),
            [d, E["sh"], *E["Pfree", u - 3]], inc="exp")

    def parts(g, c):
        u = 2 * g + c
        before = get(("pvp", u - 3))
        E["ph", u] = p.do("act", lambda e: e.activation(Ph[:, u % 3, :], P[:, u % 3, :], ACT.Copy),
                          [E["exp", g, 2 * c + 1], before], inc="ph")
        E["pl", u] = p.do("dve", lambda e: e.tensor_tensor(
            Pl[:, u % 3, :], P[:, u % 3, :], Ph[:, u % 3, :].bitcast(f32), ALU.subtract),
            [E["ph", u], before], inc="pl")
        a = p.do("pool", lambda e: e.tensor_tensor(
            A[:, c, :], P[:, u % 3, 0:512], P[:, u % 3, 512:1024], ALU.add),
            [E["exp", g, 2 * c + 1], get(("al", g - 1)), E["selr"]], inc="pa")
        E["pa", u] = a
        E["Pfree", u] = [E["ph", u], E["pl", u], a]
        if c == 1:
            a = p.do("pool", lambda e: e.tensor_tensor(A[:, 0, :], A[:, 0, :], A[:, 1, :], ALU.add),
                     [a], inc="pa")
            w = [a, get(("den", g - 2))]
            b_ = p.do("pool", lambda e: e.tensor_scalar(ah[:, g % 2, :], A[:, 0, :], 1.0, 0.0, ALU.mult, ALU.add),
                      w, inc="ah")
            E["al", g] = p.do("pool", lambda e: e.tensor_tensor(
                al[:, g % 2, :], A[:, 0, :], ah[:, g % 2, :].bitcast(f32), ALU.subtract), [b_, *w], inc="al")

    def values(g):
        q4 = g // 4
        n_, odd = g // 2, g % 2
        for c in range(2):
            u = 2 * g + c
            for j in range(2):
                jt = 2 * c + j
                v = V[:, q4 % 2, jt, (g % 4) * 128:(g % 4) * 128 + 128]
                for m, src in enumerate((Ph, Pl)):
                    w = ()
                    if j == 0 and m == 0:
                        w = [E["ph", u], E["pl", u], *E["vs", q4], get(("oadd", g - 1))]
                    d = p.do("pe", lambda e, v=v, src=src, j=j, u=u, a=(jt == 0 and m == 0),
                             z=(jt == 3 and m == 1): e.matmul(
                                 OB[:, :], v, src[:, u % 3, j * 512:(j + 1) * 512], start=a, stop=z), w,
                             inc="pv" if (j == 1 and m == 1) else None)
            E["pvp", u] = d
        E["pv", g] = d
        hi, lo = (slice(64, 128), slice(0, 64)) if odd else (slice(0, 64), slice(64, 128))
        c_ = p.do("act", lambda e: e.activation(ot[hi, :], OB[lo, :], ACT.Copy),
                  [d, get(("oadd", g - 1))], inc="ot")
        E["oadd", g] = p.do("dve", lambda e: e.tensor_tensor(
            Or[hi, n_ % 6, :], OB[hi, :], ot[hi, :], ALU.add), [c_, d, get(("nl", n_ - 6))], inc="oadd")

    def denom(g):
        h = g % 8
        s = seld[:, 112 - 16 * h:240 - 16 * h]
        w = [E["al", g], E["seld"], get(("rc", g // 8 - 1))]
        p.do("pe", lambda e: e.matmul(DB[:, :], s, ah[:, g % 2, :], start=h == 0, stop=False), w)
        E["den", g] = p.do("pe", lambda e: e.matmul(DB[:, :], s, al[:, g % 2, :], start=False, stop=h == 7),
                           inc="den")
        if h == 7:
            k = g // 8
            E["rc", k] = p.do("dve", lambda e: e.reciprocal(rc[:, :], DB[:, :]),
                              [E["den", g], get(("rl", k - 1))], inc="rc")
            w = [get(("R", 4 * k - 1))]
            E["rh", k] = p.do("act", lambda e: e.activation(rh[:, :], rc[:, :], ACT.Copy),
                              [E["rc", k], *w], inc="rh")
            E["rl", k] = p.do("dve", lambda e: e.tensor_tensor(
                rl[:, :], rc[:, :], rh[:, :].bitcast(f32), ALU.subtract), [E["rh", k], *w], inc="rl")

    def normal(n_):
        i, free = g_take()
        p.do("pe", lambda e: e.matmul(G[i][:, :], selr[:, n_ % 4, :], rh[:, :], start=True, stop=False),
             [E["rl", n_ // 4], E["selr"], *free])
        E["R", n_] = p.do("pe", lambda e: e.matmul(
            G[i][:, :], selr[:, n_ % 4, :], rl[:, :], start=False, stop=True), inc="R")
        o = Or[:, n_ % 6, :]
        a = p.do("dve", lambda e: e.tensor_tensor(o, G[i][:, :], o, ALU.mult),
                 [E["R", n_], E["oadd", 2 * n_ + 1]], inc="on")
        g_free[i] = [a]
        w = get(("out", n_ - 1))
        b_ = p.do("act", lambda e: e.activation(nh[:, :], o, ACT.Copy), [a, w], inc="nh")
        E["nl", n_] = p.do("dve", lambda e: e.tensor_tensor(nl[:, :], o, nh[:, :].bitcast(f32), ALU.subtract),
                           [b_, w], inc="nl")

    def outp(n_):
        hp = n_ % HP
        for t in range(NT):
            ts = slice(t * 128, (t + 1) * 128)
            ps = YB[t // 2][:, (t % 2) * 256:(t % 2) * 256 + 256]
            for m, (l, r) in enumerate(((nh, oh), (nl, oh), (nh, ol))):
                w = [E["nl", n_], *E["wout"], get(("yb", n_ // HP - 1))] if t == 0 and m == 0 else ()
                d = p.do("pe", lambda e, ps=ps, l=l, r=r, ts=ts, a=(hp == 0 and t % 2 == 0 and m == 0),
                         z=(hp == HP - 1 and m == 2): e.matmul(
                             ps, l[:, ts], r[:, hp, :], start=a, stop=z, skip_group_check=True), w,
                         inc="out" if (t == 3 and m == 2) else None)
        E["out", n_] = d

    def load_xr(b):
        E["xr", b] = p.dma("sp", xr[:, :, :], x[b], [get(("x1", b - 1))], inc="xr")

    y = sb("y", [128, NT, 256], f32)

    def finish(b):
        d = E["out", b * HP + HP - 1]
        for t in range(NT):
            a = p.do("dve", lambda e, t=t: e.tensor_tensor(
                y[:, t, :], YB[t // 2][:, (t % 2) * 256:(t % 2) * 256 + 256], bb[:, :], ALU.add),
                [d, E["bb"], get(("fin", b - 1))], inc="yb")
            m = stats(y[:, t, :], t, st2, mv2, [a], "ln2")
        E["yb", b] = a
        v = p.do("dve", lambda e: e.tensor_scalar_add(ve2[:, :], mv2[:, :, 1], EPS), [m], inc="ve2")
        r = p.do("pool", lambda e: e.tensor_tensor(rd2[:, :], ve2[:, :], half[:, 0:NT], ALU.pow),
                 [v], inc="rd2")
        E["fr", b] = r

    def finish2(b):
        for t in range(NT):
            a = p.do("dve", lambda e, t=t: e.tensor_scalar(
                y[:, t, :], y[:, t, :], mv2[:, t, 0:1], rd2[:, t:t + 1], ALU.subtract, ALU.mult),
                [E["fr", b]], inc="yn")
            E["fin", b] = a = p.do("dve", lambda e, t=t: e.tensor_tensor(
                xr[:, t, :], xr[:, t, :], y[:, t, :], ALU.add), [a, E["xr", b]], inc="x1r")
        E["x1", b] = p.dma("sp", x1[b], xr[:, :, :], [a], inc="x1")

    NG = B * H

    def quarter(b, q):
        return (b, q) if q < 4 else (b + 1, q - 4)

    pend = []

    def flush():
        while pend:
            qk_scale(*pend.pop(0))

    ln1(0)
    x_turn(0, 0)
    x_turn(0, 1)
    for t in range(NT):
        u = qk_tile(0, 0, t)
        flush()
        pend.append(u)
    v_tiles(0, 0, 0)
    flush()
    v_tiles(0, 0, 1)
    turn(0)

    for g in range(NG + 8):
        b, h = divmod(g, H)
        q, r = divmod(h, 4)
        live = g < NG
        nb, nq = quarter(b, q + 1)
        more = live and nb < B
        if live:
            scores(g, 0)
            scores(g, 1)
            parts(g, 0)
        if r == 1 and live:
            turn(g // 2 + 1)
        if more and r == 0:
            pend.append(qk_tile(nb, nq, 0))
        if more and r == 1:
            pend.append(qk_tile(nb, nq, 2))
        if more and r == 2:
            v_tiles(nb, nq, 0)
        if more and r == 3:
            v_tiles(nb, nq, 1)
        if live:
            scores(g, 2)
        if 1 <= g <= NG:
            values(g - 1)
        if 2 <= g <= NG + 1:
            denom(g - 2)
        if live:
            scores(g, 3)
            parts(g, 1)
        flush()
        if more and r == 0:
            pend.append(qk_tile(nb, nq, 1))
        if more and r == 1:
            pend.append(qk_tile(nb, nq, 3))
        n0 = g // 8 - 1
        k = g % 8
        if n0 >= 0 and 4 <= k <= 7:
            outp(4 * n0 + k - 4)
        if n0 >= 0 and 3 <= k <= 6:
            normal(4 * n0 + k - 3)
        if more and r == 3:
            turn(g // 2 + 1)
        if h == 7 and b >= 1:
            finish(b - 1)
        if h == 8 and b >= 1:
            finish2(b - 1)
        if b + 1 < B:
            if h == 0:
                load_x(b + 1)
            if h == 5:
                ln1(b + 1)
            if h == 11:
                x_turn(b + 1, 0)
                x_turn(b + 1, 1)
        if h == 1 and live:
            pass
        if h == 9 and live:
            load_xr(b)
        if r == 1:
            flush()
    finish2(B - 1)
    return E


def build(nc, x, wqkv, wout, bout, scale, w1, w2, h1, h2, w3, s1, s2, t1, t2, s3, out):
    f32 = mybir.dt.float32
    x1 = nc.dram_tensor("x1", (B, 128, NT, 256), f32, kind="Internal").ap()
    lows = [nc.dram_tensor("low%d" % i, s, f32, kind="Internal").ap() for i, s in enumerate((
        (128, KH, 4, 128), (128, KH, KH, 128), (128, KH, KH, 128), (128, KH, D)))]
    with ExitStack() as ctx:
        sems = {}
        p = Program()
        with ExitStack() as a:
            def sb(name, shape, dt):
                return a.enter_context(nc.sbuf_tensor(name, shape, dt))

            def pb(name, shape, dt):
                return a.enter_context(nc.psum_tensor(name, shape, dt))

            E = attention(nc, p, sb, pb, x, wqkv, wout, bout, scale, x1)
            p.do("sp", None, [E["x1", B - 1]])
            run_blocks(nc, ctx, p, sems)
        with ExitStack() as a:
            def sb(name, shape, dt):
                return a.enter_context(nc.sbuf_tensor(name, shape, dt))

            def pb(name, shape, dt):
                return a.enter_context(nc.psum_tensor(name, shape, dt))

            feed_forward(nc, p, sb, pb, x1, lows, w1, w2, h1, h2, w3, s1, s2, t1, t2, s3, out)
            run_blocks(nc, ctx, p, sems)


def feed_forward(nc, p, sb, pb, x1, lows, w1, w2, h1, h2, w3, s1, s2, t1, t2, s3, out):
    f32, f32r, i32 = mybir.dt.float32, mybir.dt.float32r, mybir.dt.int32
    ALU, ACT, AX = mybir.AluOpType, mybir.ActivationFunctionType, mybir.AxisListType
    E = {}
    get = E.get
    ADD = bass.bass_isa.ReduceOp.add

    f1 = sb("f1", [128, 2, HID], f32r)
    f2 = sb("f2", [128, 2, HID], f32r)
    f3 = sb("f3", [128, KH, HID], f32r)
    f4 = sb("f4", [128, KH, HID], f32r)
    f5 = sb("f5", [128, KH, D], f32r)
    xv = sb("xv", [128, 2, NT, D], f32)
    xn = sb("xn", [128, NT, D], f32)
    y = sb("yf", [128, NT, D], f32)
    xh = sb("xh2", [128, 2, 512], f32r)
    xl = sb("xl2", [128, 2, 512], f32r)
    hh = [sb(f"hh{i}", [128, KH, 512], f32r) for i in range(2)]
    hl = [sb(f"hl{i}", [128, KH, 512], f32r) for i in range(2)]
    stg = sb("stg", [128, 3, 1024], f32)
    R = sb("R", [128, 2, 1024], f32r)
    gg = sb("gg", [128, 2, 512], f32)
    hr = sb("hr", [128, 2, 512], f32)
    sc = {n: sb("c" + n, [128, KH], f32) for n in ("s1", "s2", "t1", "t2")}
    s3b = sb("s3b", [128, D], f32)
    ident = sb("ident2", [128, 128], f32)
    half = sb("half2", [128, 8], f32)
    cnt = sb("cnt", [128, 32], f32)
    tot = sb("tot", [128, 4], f32)
    flag = sb("flag", [128, 4], f32)
    st = sb("st3", [128, NT, 6], f32)
    mv = sb("mv3", [128, NT, 2], f32)
    ve = sb("ve3", [128, NT], f32)
    rd = sb("rd3", [128, NT], f32)
    st2 = sb("st4", [128, NT, 6], f32)
    mv2 = sb("mv4", [128, NT, 2], f32)
    ve2 = sb("ve4", [128, NT], f32)
    rd2 = sb("rd4", [128, NT], f32)

    FB = [pb(f"F{i}", [128, 512], f32) for i in range(4)]
    TB = [pb(f"T{i}", [128, 512], f32) for i in range(2)]
    WB = [pb(f"W{i}", [128, 512], f32) for i in range(2)]

    i0 = p.do("pool", lambda e: e.memset(ident[:, :], 0.0), inc="i0")
    i0 = p.do("pool", lambda e: e.memset(half[:, :], -0.5), inc="i0")
    E["ident"] = p.do("pool", lambda e: e.affine_select(
        out=ident[:, :], in_=ident[:, :], compare_op=ALU.not_equal, fill=1.0, base=0,
        pattern=[[-1, 128]], channel_multiplier=1), [i0], inc="i1")
    for n, src in (("s1", s1), ("s2", s2), ("t1", t1), ("t2", t2)):
        p.dma("act", sc[n][:, :], src, inc="cst")
    E["cst"] = p.dma("act", s3b[:, :], s3, inc="cst")

    low12, low3, low4, low5 = lows
    pieces = []
    for j, (w, f) in enumerate(((w1, f1), (w2, f2))):
        for k in range(2):
            pieces.append((0, w[:, k, :], f[:, k, :], low12[:, :, 2 * j + k, :], 8))
    for n, (w, f, low) in enumerate(((h1, f3, low3), (h2, f4, low4))):
        for k in range(KH):
            pieces.append((1 + n, w[:, k, :], f[:, k, :], low[:, :, k, :], 8))
    for k in range(2):
        pieces.append((3, w3[:, 4 * k:4 * k + 4, :], f5[:, 4 * k:4 * k + 4, :], low5[:, 4 * k:4 * k + 4, :], 4))
    at = [0]
    first_of = {0: 0, 1: 4, 2: 12, 3: 20}
    size_of = {0: 4, 1: 8, 2: 8, 3: 2}

    def load_piece(n):
        layer, w, f, low, parts_ = pieces[n]
        v = stg[:, n % 3, :]
        if parts_ == 4:
            v = v.rearrange("p (a b) -> p a b", a=4)
        E["pld", n] = p.dma("sp", v, w, [get(("plo", n - 3))], inc=f"pld{n % 3}")

    def piece():
        n = at[0]
        if n >= len(pieces):
            return
        at[0] += 1
        layer, w, f, low, parts_ = pieces[n]
        flat = stg[:, n % 3, :]
        v = flat.rearrange("p (a b) -> p a b", a=4) if parts_ == 4 else flat
        d = E["pld", n]
        a = p.do("act", lambda e: e.activation(f, v, ACT.Copy), [d], inc="fh")
        b = p.do("pool", lambda e: e.tensor_tensor(v, v, f.bitcast(f32), ALU.subtract), [a], inc="fl")
        E["cnt", n] = p.do("dve", lambda e: e.tensor_scalar(
            junk, flat, 0.0, None, ALU.not_equal, ALU.add, accum_out=cnt[:, n:n + 1]),
            [b, get(("cnt", n - 1))], inc="cnt")
        src = flat.rearrange("p (a b) -> p a b", a=parts_)
        E["plo", n] = p.dma("sp", low, src, [b, E["cnt", n]], inc=f"plo{n % 3}")
        E["low", layer] = [E["plo", m] for m in range(max(0, n - 2), n + 1)]
        E["hi", layer] = a
        if n + 3 < len(pieces):
            load_piece(n + 3)
        if n + 1 == first_of[layer] + size_of[layer]:
            c = p.do("dve", lambda e: e.reduce_sum(
                tot[:, layer:layer + 1], cnt[:, first_of[layer]:n + 1], AX.X), [E["cnt", n]], inc="tot")
            E["flag", layer] = p.do("pool", lambda e: e.partition_all_reduce(
                flag[:, layer:layer + 1], tot[:, layer:layer + 1], 128, ADD), [c], inc="flag")

    junk = gg[:, :, :].rearrange("p a b -> p (a b)")

    def load_x(b):
        E["x", b] = p.dma("sp", xv[:, b % 2, :, :], x1[b], [get(("out", b - 2))], inc=f"x1{b % 2}")

    def stats(src, t, st, mv, ready, name):
        a = p.do("dve", lambda e: e.bn_stats(st[:, t, :], src), ready, inc=name + "a")
        return p.do("dve", lambda e: e.bn_aggr(mv[:, t, :], st[:, t, :]), [a], inc=name + "b")

    def norm(b):
        for t in range(NT):
            m = stats(xv[:, b % 2, t, :], t, st, mv, [E["x", b], get(("ln", b - 1))], "ln3")
        v = p.do("dve", lambda e: e.tensor_scalar_add(ve[:, :], mv[:, :, 1], EPS), [m], inc="ve3")
        r = p.do("pool", lambda e: e.tensor_tensor(rd[:, :], ve[:, :], half[:, 0:NT], ALU.pow),
                 [v, i0], inc="rd3")
        E["rd", b] = r

    def norm2(b):
        for t in range(NT):
            E["ln", b] = p.do("dve", lambda e, t=t: e.tensor_scalar(
                xn[:, t, :], xv[:, b % 2, t, :], mv[:, t, 0:1], rd[:, t:t + 1], ALU.subtract, ALU.mult),
                [E["rd", b], get(("xT", b - 1))], inc="xn3")

    def turn(b):
        for k in range(2):
            for t in range(NT):
                d = p.do("pe", lambda e, t=t, k=k: e.transpose(
                    TB[k][:, t * 128:(t + 1) * 128], xn[:, t, k * 128:(k + 1) * 128], ident[:, :]),
                    [E["ln", b], E["ident"], get(("xs", b - 1))] if t == 0 else (),
                    inc="xT3" if t == NT - 1 else None)
            w = get(("grp", b - 1, 0, KH - 1))
            a = p.do("act", lambda e, k=k: e.activation(xh[:, k, :], TB[k][:, :], ACT.Copy), [d, w], inc="xh3")
            E["xs", b] = p.do("dve", lambda e, k=k: e.tensor_tensor(
                xl[:, k, :], TB[k][:, :], xh[:, k, :].bitcast(f32), ALU.subtract), [a, w], inc="xl3")
        E["xT", b] = d

    bank = [0]
    ffree = [None] * 4

    def chain(ps, todo, after, inc):
        for n, (l, r) in enumerate(todo):
            d = p.do("pe", lambda e, l=l, r=r, n=n: e.matmul(ps, l, r, start=n == 0, stop=n == len(todo) - 1),
                     after if n == 0 else (), inc=inc if n == len(todo) - 1 else None)
        return d

    def group(b, layer, m, banks, waits, low):
        ms = slice(m * 128, (m + 1) * 128)
        src = None if layer == 0 else (b + layer - 1) % 2
        if layer == 0:
            for j, f in enumerate((f1, f2)):
                todo = []
                for k in range(2):
                    todo += [(f[:, k, ms], xh[:, k, :]), (f[:, k, ms], xl[:, k, :])]
                    if low:
                        o = (2 * j + k) * 128
                        todo.append((R[:, m % 2, o:o + 128], xh[:, k, :]))
                d = chain(FB[banks[j]][:, :], todo, waits + low if j == 0 else (), "grp")
        else:
            f = (f3, f4)[layer - 1]
            for k in range(KH):
                todo = [(f[:, k, ms], hh[src][:, k, :]), (f[:, k, ms], hl[src][:, k, :])]
                if low:
                    todo.append((R[:, m % 2, k * 128:(k + 1) * 128], hh[src][:, k, :]))
                for n, (l, r) in enumerate(todo):
                    w = [E["h", b, layer - 1, k]] if n == 0 else []
                    if n == 0 and k == 0:
                        w = w + waits + low
                    last = k == KH - 1 and n == len(todo) - 1
                    d = p.do("pe", lambda e, l=l, r=r, a=(k == 0 and n == 0), z=last: e.matmul(
                        FB[banks[0]][:, :], l, r, start=a, stop=z), w, inc="grp" if last else None)
        E["grp", b, layer, m] = d
        return d

    def layer(b, n):
        per = 2 if n == 0 else 1
        plan = []
        for m in range(KH):
            banks = [(bank[0] + j) % 4 for j in range(per)]
            bank[0] += per
            plan.append(banks)
        return plan

    def run_layer(b, n):
        plan = layer(b, n)
        saved = dict(p.value)
        chains = 2 if n == 0 else 1
        grp0, act0, dve0 = (p.value.get(s, 0) for s in ("grp", "ea", "ed"))

        def freed(m, j):
            for e_ in range(m - 1, -1, -1):
                if j in plan[e_]:
                    return free_event(e_, j)
            return ffree[j]

        def free_event(e_, j):
            if n == 0 and j == plan[e_][1]:
                return ("ed", dve0 + e_ + 1)
            return ("ea", act0 + e_ + 1)

        def waits(m):
            w = [freed(m, j) for j in plan[m]]
            if m == 0:
                w += [E["flag", n], E["hi", n]]
                if n == 0:
                    w.append(E["xs", b])
            return w

        def fast():
            for m in range(KH):
                group(b, n, m, plan[m], waits(m), [])

        fast_ops = p.capture("pe", fast)
        after_fast = dict(p.value)

        def loads():
            for m in range(KH):
                if m >= 2:
                    w = [E["grp", b, n, m - 2]]
                else:
                    w = [E["last", b, n]] + E["low", n]
                src = low12[:, m, :, :] if n == 0 else (low3, low4)[n - 1][:, m, :, :]
                size = 512 if n == 0 else 1024
                dst = R[:, m % 2, 0:size].bitcast(f32).rearrange("p (a b) -> p a b", b=128)
                E["R", m] = p.dma("sp", dst, src, w, inc=f"R{n}{m % 2}")

        sp_ops = p.capture("sp", loads)
        p.value["grp"] = grp0

        def general():
            for m in range(KH):
                group(b, n, m, plan[m], waits(m), [E["R", m]])

        general_ops = p.capture("pe", general)
        assert p.value["grp"] == after_fast["grp"]
        word = flag[0:1, n:n + 1].bitcast(i32)
        p.do("sp", None, [E["flag", n]])
        p.branch("sp", word, sp_ops)
        p.do("pe", None, [E["flag", n]])
        p.branch("pe", word, general_ops, fast_ops)
        for m in range(KH):
            for j in plan[m]:
                ffree[j] = free_event(m, j)
        E["last", b, n + 1] = E["grp", b, n, KH - 1]
        return plan

    def evacuate(b, n, m, plan):
        dst = (b + n) % 2
        u = m % 2
        g = E["grp", b, n, m]
        if n == 0:
            w = [get(("grp", b - 1, 2, KH - 1)), get(("cnt", len(pieces) - 1)) if b else None]
            a = p.do("act", lambda e: e.activation(
                gg[:, u, :], FB[plan[m][0]][:, :], ACT.Silu, scale=sc["s1"][:, m:m + 1]),
                [g, get(("gfree", u)), E["cst"], *junked()], inc="ea")
            h = p.do("dve", lambda e: e.scalar_tensor_tensor(
                out=hr[:, u, :], in0=FB[plan[m][1]][:, :], scalar=sc["s2"][:, m:m + 1], in1=gg[:, u, :],
                op0=ALU.mult, op1=ALU.mult), [g, a, get(("hfree", u))], inc="ed")
            E["gfree", u] = h
        else:
            w = []
            s_ = sc["t1" if n == 1 else "t2"]
            h = p.do("act", lambda e: e.activation(
                hr[:, u, :], FB[plan[m][0]][:, :], ACT.Gelu, scale=s_[:, m:m + 1]),
                [g, get(("hfree", u)), E["cst"]], inc="ea")
        w = [E["last", b, n]] if n else [get(("last", b - 1, 3))]
        a = p.do("dve", lambda e: e.tensor_copy(hh[dst][:, m, :], hr[:, u, :]), [h, *w], inc="hh")
        c = p.do("dve", lambda e: e.tensor_tensor(
            hl[dst][:, m, :], hr[:, u, :], hh[dst][:, m, :].bitcast(f32), ALU.subtract), [a, *w], inc="hl")
        E["hfree", u] = c
        E["h", b, n, m] = c

    def junked():
        n = at[0] - 1
        return [get(("cnt", n))]

    def last_layer(b):
        src = b % 2
        grp0 = p.value.get("w3", 0)

        def body(low):
            for t in range(NT):
                ts = slice(t * 128, (t + 1) * 128)
                ps = WB[t // 2][:, (t % 2) * 256:(t % 2) * 256 + 256]
                for k in range(KH):
                    todo = [(hh[src][:, k, ts], f5[:, k, :]), (hl[src][:, k, ts], f5[:, k, :])]
                    if low:
                        todo.append((hh[src][:, k, ts],
                                     R[:, k // 4, (k % 4) * 256:(k % 4) * 256 + 256]))
                    for n, (l, r) in enumerate(todo):
                        w = []
                        if n == 0 and t == 0:
                            w = [E["h", b, 2, k]]
                            if k == 0:
                                w += [E["flag", 3], E["hi", 3], get(("wfree", b - 1))] + low
                        z = k == KH - 1 and n == len(todo) - 1
                        d = p.do("pe", lambda e, l=l, r=r, ps=ps, a=(k == 0 and n == 0), z=z: e.matmul(
                            ps, l, r, start=a, stop=z), w, inc="w3" if z else None)
            E["last", b, 4] = d

        fast_ops = p.capture("pe", lambda: body([]))

        def loads():
            for k in range(2):
                E["R", k] = p.dma("sp", R[:, k, :].bitcast(f32).rearrange("p (a b) -> p a b", a=4),
                                  low5[:, 4 * k:4 * k + 4, :], [E["last", b, 3]] + E["low", 3], inc=f"R3{k}")

        sp_ops = p.capture("sp", loads)
        p.value["w3"] = grp0
        general_ops = p.capture("pe", lambda: body([E["R", 0], E["R", 1]]))
        word = flag[0:1, 3:4].bitcast(i32)
        p.do("sp", None, [E["flag", 3]])
        p.branch("sp", word, sp_ops)
        p.do("pe", None, [E["flag", 3]])
        p.branch("pe", word, general_ops, fast_ops)
        E["last", b + 1, 0] = E["last", b, 4]

    def finish(b):
        for t in range(NT):
            a = p.do("dve", lambda e, t=t: e.tensor_tensor(
                y[:, t, :], WB[t // 2][:, (t % 2) * 256:(t % 2) * 256 + 256], s3b[:, :], ALU.mult),
                [E["last", b, 4], E["cst"], get(("fin", b - 1))], inc="wy")
            m = stats(y[:, t, :], t, st2, mv2, [a], "ln4")
        E["wfree", b] = a
        v = p.do("dve", lambda e: e.tensor_scalar_add(ve2[:, :], mv2[:, :, 1], EPS), [m], inc="ve4")
        E["fr", b] = p.do("pool", lambda e: e.tensor_tensor(
            rd2[:, :], ve2[:, :], half[:, 0:NT], ALU.pow), [v], inc="rd4")

    def finish2(b):
        for t in range(NT):
            a = p.do("dve", lambda e, t=t: e.tensor_scalar(
                y[:, t, :], y[:, t, :], mv2[:, t, 0:1], rd2[:, t:t + 1], ALU.subtract, ALU.mult),
                [E["fr", b]], inc="yn4")
            E["fin", b] = a = p.do("dve", lambda e, t=t: e.tensor_tensor(
                xv[:, b % 2, t, :], xv[:, b % 2, t, :], y[:, t, :], ALU.add), [a], inc="x2")
        E["out", b] = p.dma("pool", out[b], xv[:, b % 2, :, :], [a], inc=f"store{b % 2}")

    load_x(0)
    for n in range(3):
        load_piece(n)
    norm(0)
    norm2(0)
    turn(0)
    for n in range(4):
        piece()
    for b in range(B):
        E.setdefault(("last", b, 0), None)
        for n in range(3):
            plan = run_layer(b, n)
            for m in range(KH):
                evacuate(b, n, m, plan)
                if b == 0:
                    piece()
                if n == 0 and m == 1 and b:
                    finish(b - 1)
                if n == 0 and m == 3 and b:
                    finish2(b - 1)
                if n == 0 and m == 4 and b + 1 < B:
                    load_x(b + 1)
                if n == 1 and m == 2 and b + 1 < B:
                    norm(b + 1)
                if n == 1 and m == 5 and b + 1 < B:
                    norm2(b + 1)
            if n == 1 and b + 1 < B:
                turn(b + 1)
        last_layer(b)
    finish(B - 1)
    finish2(B - 1)
    p.do("pool", None, [get(("out", B - 2)), E["out", B - 1]])
    p.do("sp", None, [e for e in E["low", 3]])


def kernel(**inputs):
    import concourse.bacc as bacc
    from concourse.bass_utils import run_bass_kernel_spmd as run

    def c(a):
        return np.ascontiguousarray(a)

    g = {k.replace("L0_", ""): np.asarray(v) for k, v in inputs.items()}
    wq = g["attn_w_q"].reshape(D, 4, 2, 128)
    wk = g["attn_w_kv"][:, :H * DH].reshape(D, 4, 2, 128)
    wv = g["attn_w_kv"][:, H * DH:].reshape(D, 4, 256)
    qk = np.stack([wq, wk], axis=3).reshape(D, 4, 512)
    wqkv = np.concatenate([qk, wv], axis=2).reshape(2, 128, 4, 768).transpose(1, 0, 2, 3)

    def rows(w):
        return c(w.reshape(-1, 128, w.shape[1]).transpose(1, 0, 2))

    def cols(v):
        return c(v.reshape(-1, 128).T)

    arrays = {
        "x": c(g["attn_x"].reshape(B, NT, 128, D).transpose(0, 2, 1, 3)),
        "wqkv": c(wqkv),
        "wout": rows(g["attn_w_out"]),
        "bout": c(np.broadcast_to(g["attn_b_out"], (128, D))),
        "scale": c(np.broadcast_to(g["attn_scale"].reshape(1, H), (128, H))),
        "w1": rows(g["ffn_w1_w"].T), "w2": rows(g["ffn_w2_w"].T),
        "h1": rows(g["ffn_h1_w"].T), "h2": rows(g["ffn_h2_w"].T), "w3": rows(g["ffn_w3_w"].T),
        "s1": cols(g["ffn_w1_s"]), "s2": cols(g["ffn_w2_s"]),
        "t1": cols(g["ffn_h1_s"]), "t2": cols(g["ffn_h2_s"]),
        "s3": c(np.broadcast_to(g["ffn_w3_s"], (128, D))),
    }
    nc = bacc.Bacc("TRN2", target_bir_lowering=False, num_devices=1)
    args = [nc.dram_tensor("in_" + k, a.shape, mybir.dt.from_np(a.dtype), kind="ExternalInput").ap()
            for k, a in arrays.items()]
    o = nc.dram_tensor("out_0", (B, 128, NT, D), mybir.dt.float32, kind="ExternalOutput").ap()
    build(nc, *args, o)
    r = run(nc, [{"in_" + k: a for k, a in arrays.items()}], core_ids=[0])
    got = np.asarray(r.results[0]["out_0"])
    return c(got.transpose(0, 2, 1, 3).reshape(B, S, D))
```

```python
import concourse.bass as bass
from concourse import mybir
from contextlib import ExitStack
import numpy as np

B, S, D, H, DH = 8, 512, 256, 16, 64
HP = H // 2
NT = S // 128
HID = 1024
KH = HID // 128
EPS = 1e-5
TINY = 1e-24
TOP = 80.0


class Program:

    def __init__(self):
        self.ops = {"pe": [], "act": [], "dve": [], "pool": [], "sp": []}
        self.value = {}

    def do(self, engine, fn, after=(), inc=None, by=1):
        self.ops[engine].append((fn, [e for e in after if e is not None], inc, by))
        if inc is None:
            return None
        self.value[inc] = self.value.get(inc, 0) + by
        return (inc, self.value[inc])

    def dma(self, engine, out, in_, after=(), inc=None):
        return self.do(engine, lambda e: e.dma_start(out, in_), after, inc, 16)

    def capture(self, engine, build):
        kept, self.ops[engine] = self.ops[engine], []
        build()
        taken, self.ops[engine] = self.ops[engine], kept
        return taken

    def branch(self, engine, flag, nonzero, zero=()):
        self.ops[engine].append((flag, nonzero, zero))

    def issue(self, name, engine, sems, reached):
        self.put(self.ops[name], engine, sems, reached)
        self.ops[name] = []

    def put(self, ops, engine, sems, reached):
        for op in ops:
            if len(op) == 3:
                flag, nonzero, zero = op
                word = engine.value_load(flag)
                with engine.If(word != 0):
                    self.put(nonzero, engine, sems, dict(reached))
                if zero:
                    with engine.Else():
                        self.put(zero, engine, sems, dict(reached))
                continue
            fn, after, inc, by = op
            for sem, value in after:
                if reached.get(sem, 0) < value:
                    engine.wait_ge(sems[sem], value)
                    reached[sem] = value
            if fn is None:
                continue
            done = fn(engine)
            if inc is not None:
                done.then_inc(sems[inc], by)


def run_blocks(nc, ctx, p, sems):
    for s in sorted(p.value):
        if s not in sems:
            sems[s] = ctx.enter_context(nc.semaphore("s_" + s))
    with nc.Block() as block:
        @block.sync
        def _(e):
            p.issue("sp", e, sems, {})

        @block.gpsimd
        def _(e):
            p.issue("pool", e, sems, {})

        @block.scalar
        def _(e):
            p.issue("act", e, sems, {})

        @block.vector
        def _(e):
            p.issue("dve", e, sems, {})

        @block.tensor
        def _(e):
            p.issue("pe", e, sems, {})


def attention(nc, p, sb, pb, x, wqkv, wout, bout, scale, x1):
    f32, f32r = mybir.dt.float32, mybir.dt.float32r
    ALU, ACT, AX = mybir.AluOpType, mybir.ActivationFunctionType, mybir.AxisListType
    E = {}
    get = E.get

    wh = sb("wh", [128, 2, 4, 768], f32r)
    wl = sb("wl", [128, 2, 4, 768], f32r)
    oh = sb("oh", [128, HP, 256], f32r)
    ol = sb("ol", [128, HP, 256], f32r)
    xt = sb("xt", [128, NT, 256], f32)
    xr = sb("xr", [128, NT, 256], f32)
    y = sb("y", [128, NT, 256], f32)
    xh = sb("xh", [128, 2, 512], f32r)
    xl = sb("xl", [128, 2, 512], f32r)
    qk = sb("qk", [128, 3, NT, 256], f32)
    th = sb("th", [128, 2, 2, 512], f32r)
    tl = sb("tl", [128, 2, 2, 512], f32r)
    V = sb("V", [128, 2, NT, 512], f32r)
    P = sb("P", [128, 3, 1024], f32)
    Ph = sb("Ph", [128, 3, 1024], f32r)
    Pl = sb("Pl", [128, 3, 1024], f32r)
    A = sb("A", [128, 2, 512], f32)
    ah = sb("ah", [128, 2, 512], f32r)
    al = sb("al", [128, 2, 512], f32r)
    ot = sb("ot", [128, 512], f32)
    Or = sb("Or", [128, 6, 512], f32)
    rc = sb("rc", [128, 512], f32)
    rh = sb("rh", [128, 512], f32r)
    rl = sb("rl", [128, 512], f32r)
    nh = sb("nh", [128, 512], f32r)
    nl = sb("nl", [128, 512], f32r)
    sq = sb("sq", [128, 512], f32)
    ident = sb("ident", [128, 128], f32)
    seld = sb("seld", [128, 240], f32r)
    selr = sb("selr", [128, 4, 128], f32r)
    bb = sb("bb", [128, 256], f32)
    es = sb("es", [128, H], f32)
    sh = sb("sh", [128, H], f32)
    eq = sb("eq", [128, 4, 2, 2, 2], f32)
    half = sb("half", [128, 8], f32)
    ss = sb("ss", [128, 2, 8], f32)
    rs = sb("rs", [128, 2, 8], f32)
    st = sb("st", [128, NT, 6], f32)
    mv = sb("mv", [128, NT, 2], f32)
    ve = sb("ve", [128, NT], f32)
    rd = sb("rd", [128, NT], f32)
    st2 = sb("st2", [128, NT, 6], f32)
    mv2 = sb("mv2", [128, NT, 2], f32)
    ve2 = sb("ve2", [128, NT], f32)
    rd2 = sb("rd2", [128, NT], f32)

    SB = [pb(f"S{i}", [128, 512], f32) for i in range(2)]
    G = [pb(f"G{i}", [128, 512], f32) for i in range(2)]
    OB = pb("OB", [128, 512], f32)
    DB = pb("DB", [128, 512], f32)
    YB = [pb(f"Y{i}", [128, 512], f32) for i in range(2)]

    p.do("pool", lambda e: e.memset(ident[:, :], 0.0), inc="c0")
    p.do("pool", lambda e: e.memset(half[:, :], -0.5), inc="c0")
    p.do("pool", lambda e: e.memset(A[:, :, :], 0.0), inc="c0")
    c0 = p.do("pool", lambda e: e.memset(P[:, 0, 0:240], 0.0), inc="c0")
    E["ident"] = p.do("pool", lambda e: e.affine_select(
        out=ident[:, :], in_=ident[:, :], compare_op=ALU.not_equal, fill=1.0, base=0,
        pattern=[[-1, 128]], channel_multiplier=1), [c0], inc="c1")
    c2 = p.do("pool", lambda e: e.memset(P[:, 0, 112:128], 1.0), [c0], inc="c1")
    c3 = p.do("pool", lambda e: e.affine_select(
        out=A[:, 0, :].rearrange("p (b c d) -> p b c d", b=4, c=2),
        in_=A[:, 0, :].rearrange("p (b c d) -> p b c d", b=4, c=2),
        compare_op=ALU.not_equal, fill=1.0, base=0,
        pattern=[[-32, 4], [-16, 2], [0, 64]], channel_multiplier=1), [c0], inc="c1")
    E["seld"] = p.do("dve", lambda e: e.tensor_copy(seld[:, :], P[:, 0, 0:240]), [c2], inc="c2")
    E["selr"] = p.do("dve", lambda e: e.tensor_copy(
        selr[:, :, :].rearrange("p a b -> p (a b)"), A[:, 0, :]),
        [c3], inc="c2")
    E["bb"] = p.dma("act", bb[:, :], bout, inc="bb")
    ld = p.dma("act", es[:, :], scale, inc="sc")
    E["es"] = p.do("act", lambda e: e.activation(es[:, :], es[:, :], ACT.Exp), [ld], inc="es")
    eq0 = p.do("dve", lambda e: e.memset(eq[:, :, :, :, :].rearrange("p a b c d -> p (a b c d)"), 1.0),
               inc="eq")
    for j in range(2):
        E["eq"] = p.do("dve", lambda e, j=j: e.tensor_copy(
            eq[:, :, j, 0, :], es[:, :].rearrange("p (a b d) -> p a b d", a=4, b=2)[:, :, j, :]),
            [eq0, E["es"]], inc="eq")
    sh0 = p.do("dve", lambda e: e.tensor_scalar(sh[:, :], es[:, :], -1.0, TOP, ALU.mult, ALU.add),
               [E["es"]], inc="sh")
    E["sh"] = p.do("dve", lambda e: e.tensor_scalar_min(sh[:, :], sh[:, :], 0.0), [sh0], inc="sh")

    g_at = [0]
    g_free = [[], []]

    def g_take():
        i = g_at[0] % 2
        g_at[0] += 1
        return i, g_free[i]

    def split(psum, hi, lo, after, name, free=()):
        a = p.do("act", lambda e: e.activation(hi, psum, ACT.Copy), [after, *free], inc=name + "h")
        b = p.do("dve", lambda e: e.tensor_tensor(lo, psum, hi.bitcast(f32), ALU.subtract),
                 [a, *free], inc=name + "l")
        return a, b

    E["x", 0] = p.dma("sp", xt[:, :, :], x[0], inc="x")
    of = Or[:, :, :].rearrange("p a b -> p (a b)")
    stage = ([P[:, i, 0:768] for i in range(3)] + [of[:, i * 768:(i + 1) * 768] for i in range(4)]
             + [A[:, :, :].rearrange("p a b -> p (a b)")[:, 0:768]])
    wld = {}

    def load_w(n):
        wait = {0: [E["seld"]], 7: [E["selr"]]}.get(n, [])
        wld[n] = p.dma("sp", stage[n], wqkv[:, n % 2, n // 2, :], wait, inc=f"wld{n}")

    def split_w(n):
        q, k = divmod(n, 2)
        a = p.do("act", lambda e: e.activation(wh[:, k, q, :], stage[n], ACT.Copy), [wld[n]], inc="wh")
        b = p.do("dve", lambda e: e.tensor_tensor(
            wl[:, k, q, :], stage[n], wh[:, k, q, :].bitcast(f32), ALU.subtract), [a], inc="wl")
        E["w", q] = E["wlast"] = [a, b]

    ostage = [t_[:, :, :] for t_ in (y, xr)]

    def load_wo(k):
        wld["o", k] = p.dma("sp", ostage[k], wout[:, 4 * k:4 * k + 4, :], inc=f"wldo{k}")

    def split_wo(k):
        o = slice(4 * k, 4 * k + 4)
        a = p.do("act", lambda e: e.activation(oh[:, o, :], ostage[k], ACT.Copy), [wld["o", k]], inc="wh")
        b = p.do("dve", lambda e: e.tensor_tensor(
            ol[:, o, :], ostage[k], oh[:, o, :].bitcast(f32), ALU.subtract), [a], inc="wl")
        E["wout"] = E["wolast"] = [a, b]

    for n in range(8):
        load_w(n)
    for k in range(2):
        load_wo(k)
    for i in range(3):
        E["Pfree", i - 3] = ()

    def load_x(b):
        E["x", b] = p.dma("sp", xt[:, :, :], x[b], [get(("xT", b - 1))], inc="x")

    def stats(src, t, st, mv, ready, name):
        a = p.do("dve", lambda e: e.bn_stats(st[:, t, :], src), ready, inc=name + "a")
        return p.do("dve", lambda e: e.bn_aggr(mv[:, t, :], st[:, t, :]), [a], inc=name + "b")

    def ln1(b, t):
        m = stats(xt[:, t, :], t, st, mv, [E["x", b], get(("ln", b - 1))], "ln1")
        if t == NT - 1:
            v = p.do("dve", lambda e: e.tensor_scalar_add(ve[:, :], mv[:, :, 1], EPS), [m], inc="ve")
            E["rd", b] = p.do("pool", lambda e: e.tensor_tensor(
                rd[:, :], ve[:, :], half[:, 0:NT], ALU.pow), [v, c0], inc="rd")

    def ln1b(b, t):
        E["ln", b] = p.do("dve", lambda e: e.tensor_scalar(
            xt[:, t, :], xt[:, t, :], mv[:, t, 0:1], rd[:, t:t + 1], ALU.subtract, ALU.mult),
            [E["rd", b]], inc="xn")

    def x_turn(b, k):
        i, free = g_take()
        for t in range(NT):
            d = p.do("pe", lambda e, t=t: e.transpose(
                G[i][:, t * 128:(t + 1) * 128], xt[:, t, k * 128:(k + 1) * 128], ident[:, :]),
                [E["ln", b], E["ident"], *free] if t == 0 else (), inc="xT" if t == NT - 1 else None)
        E["xT", b] = d
        g_free[i] = split(G[i][:, :], xh[:, k, :], xl[:, k, :], d, "x", [get(("v", b - 1, 3))])
        E["xs", b] = g_free[i]

    def terms(ps, ah_, al_, bh, bl, first, last):
        todo = [(ah_, bh), (al_, bh), (ah_, bl)]
        for n_, (l, r) in enumerate(todo):
            yield (lambda e, l=l, r=r, n_=n_: e.matmul(
                ps, l, r, start=first and n_ == 0, stop=last and n_ == 2, skip_group_check=True))

    def project(b, q, t, c0_, c1_, ps, after, inc):
        fns = []
        for k in range(2):
            xs = slice(t * 128, (t + 1) * 128)
            fns += list(terms(ps, xh[:, k, xs], xl[:, k, xs], wh[:, k, q, c0_:c1_], wl[:, k, q, c0_:c1_],
                              k == 0, k == 1))
        for n_, fn in enumerate(fns):
            d = p.do("pe", fn, after if n_ == 0 else (), inc=inc if n_ == len(fns) - 1 else None)
        return d

    def qk_tile(b, q, t):
        i, free = g_take()
        d = project(b, q, t, 0, 512, G[i][:, :], [*E["xs", b], *E["w", q], *free], "qk")
        hp = b * HP + 2 * q
        u = (b * 4 + q) * NT + t
        for j in range(2):
            n_ = hp + j
            c = p.do("act", lambda e, j=j, n_=n_: e.activation(
                qk[:, n_ % 3, t, :], G[i][:, j * 256:(j + 1) * 256], ACT.Copy),
                [d, get(("T", n_ - 3))], inc="qkc")
        s = p.do("act", lambda e: e.activation(sq[:, :], G[i][:, :], ACT.Square),
                 [get(("ssum", u - 1))], inc="sq")
        g_free[i] = [s]
        m0 = p.do("dve", lambda e: e.reduce_sum(
            ss[:, u % 2, :], sq[:, :].rearrange("p (h d) -> p h d", d=DH), AX.X),
            [s, get(("rs", u - 2))], inc="ssum")
        E["ssum", u] = m0
        m1 = p.do("dve", lambda e: e.tensor_scalar_max(ss[:, u % 2, :], ss[:, u % 2, :], TINY),
                  [m0], inc="smax")
        E["rs", u] = p.do("pool", lambda e: e.tensor_tensor(
            rs[:, u % 2, :], ss[:, u % 2, :], half[:, :], ALU.pow), [m1, get(("qkn", u - 2))], inc="rs")
        return u, hp, q, t, c

    def qk_scale(u, hp, q, t, c):
        f = p.do("dve", lambda e: e.tensor_tensor(
            rs[:, u % 2, :], rs[:, u % 2, :], eq[:, q, :, :, :].rearrange("p b c d -> p (b c d)"), ALU.mult),
            [E["rs", u], E["eq"]], inc="rq")
        for j in range(2):
            a = qk[:, (hp + j) % 3, t, :].rearrange("p (h d) -> p h d", d=DH)
            r = rs[:, u % 2, 4 * j:4 * j + 4].unsqueeze(2).to_broadcast([128, 4, DH])
            E["qkn", u] = E["qkr", hp + j] = p.do(
                "dve", lambda e, a=a, r=r: e.tensor_tensor(a, a, r, ALU.mult), [f, c], inc="qkn")

    def v_tiles(b, q, half_):
        i, free = g_take()
        s = (b * 4 + q) % 2
        for t in (2 * half_, 2 * half_ + 1):
            o = (t % 2) * 256
            d = project(b, q, t, 512, 768, G[i][:, o:o + 256],
                        [*E["xs", b], *free] if t % 2 == 0 else (), "v")
        prev = b * 4 + q - 2
        w = [d, get(("pv", 4 * prev + 3))]
        moves = []
        for t in (2 * half_, 2 * half_ + 1):
            o = (t % 2) * 256
            src = G[i][:, o:o + 256].rearrange("p (a b d) -> p a b d", a=2, b=2)
            vv = V[:, s, t, :].rearrange("p (a s d) -> p a s d", a=2, s=4)
            for b_ in range(2):
                moves.append((src[:, :, b_, :], vv[:, :, 3 * b_, :], vv[:, :, 1 + b_, :]))
        for src, hi, lo in moves:
            x_ = p.do("act", lambda e, src=src, hi=hi: e.activation(hi, src, ACT.Copy), w, inc="vh")
        for src, hi, lo in moves:
            y_ = p.do("dve", lambda e, src=src, hi=hi, lo=lo: e.tensor_tensor(
                lo, src, hi.bitcast(f32), ALU.subtract), [x_, *w], inc="vl")
        g_free[i] = [x_, y_]
        E["v", b, q] = d
        E["vs", b * 4 + q] = [x_, y_]

    def turn(n_, which):
        for j in which:
            i, free = g_take()
            for t in range(NT):
                d = p.do("pe", lambda e, i=i, j=j, t=t: e.transpose(
                    G[i][:, t * 128:(t + 1) * 128], qk[:, n_ % 3, t, j * 128:(j + 1) * 128], ident[:, :]),
                    [E["qkr", n_], *free] if t == 0 else (), inc="T" if t == NT - 1 else None)
            g_free[i] = split(G[i][:, :], th[:, n_ % 2, j, :], tl[:, n_ % 2, j, :], d, "t",
                              [get(("s", 2 * (n_ - 2) + 1, NT - 1))])
            E["T", n_] = d
            E["ts", n_] = g_free[i]

    def scores(g, jt):
        n_, r = g // 2, 64 * (g % 2)
        b_ = (NT * g + jt) % 2
        js = slice(jt * 128, (jt + 1) * 128)
        kh, kl = th[r:r + 64, n_ % 2, 1, js], tl[r:r + 64, n_ % 2, 1, js]
        qh, ql = th[r:r + 64, n_ % 2, 0, :], tl[r:r + 64, n_ % 2, 0, :]
        before = get(("exp", g, jt - 2)) if jt >= 2 else get(("exp", g - 1, jt + 2))
        for m, fn in enumerate(terms(SB[b_][:, :], kh, kl, qh, ql, True, True)):
            d = p.do("pe", fn, [*E["ts", n_], before] if m == 0 else (), inc="s" if m == 2 else None)
        E["s", g, jt] = d
        h = g % H
        u = 2 * g + jt // 2
        c = (jt % 2) * 512
        E["exp", g, jt] = p.do("act", lambda e: e.activation(
            P[:, u % 3, c:c + 512], SB[b_][:, :], ACT.Exp, bias=sh[:, h:h + 1]),
            [d, E["sh"], *E["Pfree", u - 3], *E["wlast"]], inc="exp")

    def parts(u):
        g, c = divmod(u, 2)
        before = get(("pvp", u - 3))
        E["ph", u] = p.do("act", lambda e: e.activation(Ph[:, u % 3, :], P[:, u % 3, :], ACT.Copy),
                          [E["exp", g, 2 * c + 1], before], inc="ph")
        E["pl", u] = p.do("dve", lambda e: e.tensor_tensor(
            Pl[:, u % 3, :], P[:, u % 3, :], Ph[:, u % 3, :].bitcast(f32), ALU.subtract),
            [E["ph", u], before], inc="pl")
        a = p.do("pool", lambda e: e.tensor_tensor(
            A[:, c, :], P[:, u % 3, 0:512], P[:, u % 3, 512:1024], ALU.add),
            [E["exp", g, 2 * c + 1], get(("al", g - 1)), *E["wlast"]], inc="pa")
        E["Pfree", u] = [E["ph", u], E["pl", u], a]
        if c == 1:
            a = p.do("pool", lambda e: e.tensor_tensor(A[:, 0, :], A[:, 0, :], A[:, 1, :], ALU.add),
                     [a], inc="pa")
            w = [a, get(("den", g - 2))]
            b_ = p.do("pool", lambda e: e.tensor_scalar(
                ah[:, g % 2, :], A[:, 0, :], 1.0, 0.0, ALU.mult, ALU.add), w, inc="ah")
            E["al", g] = p.do("pool", lambda e: e.tensor_tensor(
                al[:, g % 2, :], A[:, 0, :], ah[:, g % 2, :].bitcast(f32), ALU.subtract),
                [b_, *w], inc="al")

    def values(u):
        g, c = divmod(u, 2)
        q4, n_ = g // 4, g // 2
        for j in range(2):
            jt = 2 * c + j
            v = V[:, q4 % 2, jt, (g % 4) * 128:(g % 4) * 128 + 128]
            for m, src in enumerate((Ph, Pl)):
                w = ()
                if j == 0 and m == 0:
                    w = [E["ph", u], E["pl", u], *E["vs", q4], get(("oadd", g - 1))]
                d = p.do("pe", lambda e, v=v, src=src, j=j, a=(jt == 0 and m == 0),
                         z=(jt == 3 and m == 1): e.matmul(
                             OB[:, :], v, src[:, u % 3, j * 512:(j + 1) * 512], start=a, stop=z), w,
                         inc="pv" if (j == 1 and m == 1) else None)
        E["pvp", u] = E["pv", g] = d
        if c == 1:
            hi, lo = (slice(64, 128), slice(0, 64)) if g % 2 else (slice(0, 64), slice(64, 128))
            c_ = p.do("act", lambda e: e.activation(ot[hi, :], OB[lo, :], ACT.Copy),
                      [d, get(("oadd", g - 1))], inc="ot")
            E["oadd", g] = p.do("dve", lambda e: e.tensor_tensor(
                Or[hi, n_ % 6, :], OB[hi, :], ot[hi, :], ALU.add), [c_, d, get(("nl", n_ - 6)), *E["wlast"]], inc="oadd")

    def denom(g):
        h = g % 8
        s = seld[:, 112 - 16 * h:240 - 16 * h]
        w = [E["al", g], E["seld"], get(("rc", g // 8 - 1))]
        p.do("pe", lambda e: e.matmul(DB[:, :], s, ah[:, g % 2, :], start=h == 0, stop=False), w)
        E["den", g] = p.do("pe", lambda e: e.matmul(DB[:, :], s, al[:, g % 2, :], start=False, stop=h == 7),
                           inc="den")

    def take_sums(k):
        E["rs0", k] = p.do("act", lambda e: e.activation(rc[:, :], DB[:, :], ACT.Copy),
                           [E["den", 8 * k + 7], get(("rl", k - 1))], inc="rc0")
        E["rc", k] = E["rs0", k]

    def invert(k, j):
        cs = slice(j * 128, (j + 1) * 128)
        a = p.do("dve", lambda e: e.reciprocal(rc[:, cs], rc[:, cs]), [E["rs0", k]], inc="rc")
        if j == 3:
            w = [get(("R", 4 * k - 1))]
            b_ = p.do("act", lambda e: e.activation(rh[:, :], rc[:, :], ACT.Copy), [a, *w], inc="rh")
            E["rl", k] = p.do("dve", lambda e: e.tensor_tensor(
                rl[:, :], rc[:, :], rh[:, :].bitcast(f32), ALU.subtract), [b_, *w], inc="rl")

    def normal(n_):
        i, free = g_take()
        p.do("pe", lambda e: e.matmul(G[i][:, :], selr[:, n_ % 4, :], rh[:, :], start=True, stop=False),
             [E["rl", n_ // 4], E["selr"], *free])
        E["R", n_] = p.do("pe", lambda e: e.matmul(
            G[i][:, :], selr[:, n_ % 4, :], rl[:, :], start=False, stop=True), inc="R")
        o = Or[:, n_ % 6, :]
        a = p.do("dve", lambda e: e.tensor_tensor(o, G[i][:, :], o, ALU.mult),
                 [E["R", n_], E["oadd", 2 * n_ + 1]], inc="on")
        g_free[i] = [a]
        E["on", n_] = a

    def normal2(n_):
        o = Or[:, n_ % 6, :]
        a = E["on", n_]
        w = get(("out", n_ - 1))
        b_ = p.do("act", lambda e: e.activation(nh[:, :], o, ACT.Copy), [a, w], inc="nh")
        E["nl", n_] = p.do("dve", lambda e: e.tensor_tensor(nl[:, :], o, nh[:, :].bitcast(f32), ALU.subtract),
                           [b_, w], inc="nl")

    def outp(n_):
        hp = n_ % HP
        for t in range(NT):
            ts = slice(t * 128, (t + 1) * 128)
            ps = YB[t // 2][:, (t % 2) * 256:(t % 2) * 256 + 256]
            for m, (l, r) in enumerate(((nh, oh), (nl, oh), (nh, ol))):
                w = [E["nl", n_], *E["wout"], get(("yb", n_ // HP - 1))] if t == 0 and m == 0 else ()
                d = p.do("pe", lambda e, ps=ps, l=l, r=r, ts=ts, a=(hp == 0 and t % 2 == 0 and m == 0),
                         z=(hp == HP - 1 and m == 2): e.matmul(
                             ps, l[:, ts], r[:, hp, :], start=a, stop=z, skip_group_check=True), w,
                         inc="out" if (t == 3 and m == 2) else None)
        E["out", n_] = d

    def load_xr(b):
        E["xr", b] = p.dma("sp", xr[:, :, :], x[b], [get(("x1", b - 1)), *E["wolast"]], inc="xr")

    def finish(b, t):
        a = p.do("dve", lambda e: e.tensor_tensor(
            y[:, t, :], YB[t // 2][:, (t % 2) * 256:(t % 2) * 256 + 256], bb[:, :], ALU.add),
            [E["out", b * HP + HP - 1], E["bb"], get(("fin", b - 1)), *E["wolast"]], inc="yb")
        m = stats(y[:, t, :], t, st2, mv2, [a], "ln2")
        if t == NT - 1:
            E["yb", b] = a
            v = p.do("dve", lambda e: e.tensor_scalar_add(ve2[:, :], mv2[:, :, 1], EPS), [m], inc="ve2")
            E["fr", b] = p.do("pool", lambda e: e.tensor_tensor(
                rd2[:, :], ve2[:, :], half[:, 0:NT], ALU.pow), [v], inc="rd2")

    def finish2(b, t):
        a = p.do("dve", lambda e: e.tensor_scalar(
            y[:, t, :], y[:, t, :], mv2[:, t, 0:1], rd2[:, t:t + 1], ALU.subtract, ALU.mult),
            [E["fr", b]], inc="yn")
        E["fin", b] = a = p.do("dve", lambda e: e.tensor_tensor(
            xr[:, t, :], xr[:, t, :], y[:, t, :], ALU.add), [a, E["xr", b]], inc="x1r")
        if t == NT - 1:
            E["x1", b] = p.dma("sp", x1[b], xr[:, :, :], [a], inc="x1")

    NU = 2 * B * H
    pend = {}

    def later(i, fn, *args):
        pend.setdefault(i, []).append((fn, args))

    for t in range(NT):
        ln1(0, t)
    for t in range(NT):
        ln1b(0, t)
    x_turn(0, 0)
    x_turn(0, 1)
    split_w(0)
    split_w(1)
    prev = None
    for t in range(NT):
        u = qk_tile(0, 0, t)
        if prev:
            qk_scale(*prev)
        prev = u
    v_tiles(0, 0, 0)
    qk_scale(*prev)
    split_w(2)
    turn(0, (0, 1))
    split_w(3)
    v_tiles(0, 0, 1)
    split_w(7)

    for i in range(NU + 25):
        g, c = divmod(i, 2)
        live = i < NU
        b, h = divmod(g, H)
        r = i % 8
        nb, nq = (b, h // 4 + 1) if h < 12 else (b + 1, 0)
        more = live and nb < B
        i16, k8 = i % 16, i // 16 - 1
        if live:
            scores(g, 2 * c)
            scores(g, 2 * c + 1)
        if 0 <= i - 3 < NU:
            values(i - 3)
        if 0 <= i - 1 < NU:
            parts(i - 1)
        if i16 in (11, 13, 15) and 0 <= k8 < 2 * B:
            outp(4 * k8 + (i16 - 11) // 2)
        if i16 == 1 and 1 <= k8 <= 2 * B:
            outp(4 * k8 - 1)
        if i < 3:
            split_w(4 + i)
        if i in (5, 6):
            split_wo(i - 5)
        for fn, args in pend.pop(i, []):
            fn(*args)
        if more and r < 4:
            later(i + 1, qk_scale, *qk_tile(nb, nq, r))
        if live and r in (0, 1):
            turn(g // 2 + 1 if r == 0 else i // 4 + 1, (r,))
        if more and (r == 4 or r == (5 if nq == 3 else 7)):
            v_tiles(nb, nq, r // 5)
        if more and r in (5, 6):
            turn(i // 4 + 1, (r - 5,))
        if 0 <= k8 < 2 * B and i16 == 4:
            take_sums(k8)
        if 0 <= k8 < 2 * B and i16 in (4, 5, 6, 7):
            invert(k8, i16 - 4)
        if c == 1 and 0 <= g - 2 < B * H:
            denom(g - 2)
        if i16 in (8, 10, 12, 14) and 0 <= k8 < 2 * B:
            n_ = 4 * k8 + (i16 - 8) // 2
            normal(n_)
            later(i + 1, normal2, n_)
        i32, pb_ = i % 32, i // 32 - 1
        if 0 <= pb_ < B:
            if i32 in (17, 18, 19, 20):
                finish(pb_, i32 - 17)
            if i32 in (21, 22, 23, 24):
                finish2(pb_, i32 - 21)
        if b + 1 < B:
            if i32 == 0:
                load_x(b + 1)
            if i32 in (8, 9, 10, 11):
                ln1(b + 1, i32 - 8)
            if i32 in (13, 14, 15, 16):
                ln1b(b + 1, i32 - 13)
            if i32 == 22:
                x_turn(b + 1, 0)
            if i32 == 23:
                x_turn(b + 1, 1)
        if live and i32 == 28:
            load_xr(b)
    return E


def build(nc, x, wqkv, wout, bout, scale, w1, w2, h1, h2, w3, s1, s2, t1, t2, s3, out):
    f32 = mybir.dt.float32
    x1 = nc.dram_tensor("x1", (B, 128, NT, 256), f32, kind="Internal").ap()
    lows = [nc.dram_tensor("low%d" % i, s, f32, kind="Internal").ap() for i, s in enumerate((
        (128, KH, 4, 128), (128, KH, KH, 128), (128, KH, KH, 128), (128, KH, D)))]
    with ExitStack() as ctx:
        sems = {}
        p = Program()
        with ExitStack() as a:
            def sb(name, shape, dt):
                return a.enter_context(nc.sbuf_tensor(name, shape, dt))

            def pb(name, shape, dt):
                return a.enter_context(nc.psum_tensor(name, shape, dt))

            E = attention(nc, p, sb, pb, x, wqkv, wout, bout, scale, x1)
            p.do("sp", None, [E["x1", B - 1]])
            run_blocks(nc, ctx, p, sems)
        with ExitStack() as a:
            def sb(name, shape, dt):
                return a.enter_context(nc.sbuf_tensor(name, shape, dt))

            def pb(name, shape, dt):
                return a.enter_context(nc.psum_tensor(name, shape, dt))

            feed_forward(nc, p, sb, pb, x1, lows, w1, w2, h1, h2, w3, s1, s2, t1, t2, s3, out)
            run_blocks(nc, ctx, p, sems)


def feed_forward(nc, p, sb, pb, x1, lows, w1, w2, h1, h2, w3, s1, s2, t1, t2, s3, out):
    f32, f32r, i32 = mybir.dt.float32, mybir.dt.float32r, mybir.dt.int32
    ALU, ACT, AX = mybir.AluOpType, mybir.ActivationFunctionType, mybir.AxisListType
    E = {}
    get = E.get
    ADD = bass.bass_isa.ReduceOp.add

    f1 = sb("f1", [128, 2, HID], f32r)
    f2 = sb("f2", [128, 2, HID], f32r)
    f3 = sb("f3", [128, KH, HID], f32r)
    f4 = sb("f4", [128, KH, HID], f32r)
    f5 = sb("f5", [128, KH, D], f32r)
    xv = sb("xv", [128, 2, NT, D], f32)
    xn = sb("xn", [128, NT, D], f32)
    y = sb("yf", [128, NT, D], f32)
    xh = sb("xh2", [128, 2, 512], f32r)
    xl = sb("xl2", [128, 2, 512], f32r)
    hh = [sb(f"hh{i}", [128, KH, 512], f32r) for i in range(2)]
    hl = [sb(f"hl{i}", [128, KH, 512], f32r) for i in range(2)]
    stg = sb("stg", [128, 3, 1024], f32)
    R = sb("R", [128, 2, 1024], f32r)
    gg = sb("gg", [128, 2, 512], f32)
    hr = sb("hr", [128, 2, 512], f32)
    sc = {n: sb("c" + n, [128, KH], f32) for n in ("s1", "s2", "t1", "t2")}
    s3b = sb("s3b", [128, D], f32)
    ident = sb("ident2", [128, 128], f32)
    half = sb("half2", [128, 8], f32)
    cnt = sb("cnt", [128, 32], f32)
    tot = sb("tot", [128, 4], f32)
    flag = sb("flag", [128, 4], f32)
    st = sb("st3", [128, NT, 6], f32)
    mv = sb("mv3", [128, NT, 2], f32)
    ve = sb("ve3", [128, NT], f32)
    rd = sb("rd3", [128, NT], f32)
    st2 = sb("st4", [128, NT, 6], f32)
    mv2 = sb("mv4", [128, NT, 2], f32)
    ve2 = sb("ve4", [128, NT], f32)
    rd2 = sb("rd4", [128, NT], f32)

    FB = [pb(f"F{i}", [128, 512], f32) for i in range(4)]
    TB = [pb(f"T{i}", [128, 512], f32) for i in range(2)]
    WB = [pb(f"W{i}", [128, 512], f32) for i in range(2)]

    i0 = p.do("pool", lambda e: e.memset(ident[:, :], 0.0), inc="i0")
    i0 = p.do("pool", lambda e: e.memset(half[:, :], -0.5), inc="i0")
    E["ident"] = p.do("pool", lambda e: e.affine_select(
        out=ident[:, :], in_=ident[:, :], compare_op=ALU.not_equal, fill=1.0, base=0,
        pattern=[[-1, 128]], channel_multiplier=1), [i0], inc="i1")
    for n, src in (("s1", s1), ("s2", s2), ("t1", t1), ("t2", t2)):
        p.dma("act", sc[n][:, :], src, inc="cst")
    E["cst"] = p.dma("act", s3b[:, :], s3, inc="cst")

    low12, low3, low4, low5 = lows
    pieces = []
    for j, (w, f) in enumerate(((w1, f1), (w2, f2))):
        for k in range(2):
            pieces.append((0, w[:, k, :], f[:, k, :], low12[:, :, 2 * j + k, :], 8))
    for n, (w, f, low) in enumerate(((h1, f3, low3), (h2, f4, low4))):
        for k in range(KH):
            pieces.append((1 + n, w[:, k, :], f[:, k, :], low[:, :, k, :], 8))
    for k in range(2):
        pieces.append((3, w3[:, 4 * k:4 * k + 4, :], f5[:, 4 * k:4 * k + 4, :], low5[:, 4 * k:4 * k + 4, :], 4))
    at = [0]
    first_of = {0: 0, 1: 4, 2: 12, 3: 20}
    size_of = {0: 4, 1: 8, 2: 8, 3: 2}

    def load_piece(n):
        layer, w, f, low, parts_ = pieces[n]
        v = stg[:, n % 3, :]
        if parts_ == 4:
            v = v.rearrange("p (a b) -> p a b", a=4)
        E["pld", n] = p.dma("sp", v, w, [get(("plo", n - 3))], inc=f"pld{n % 3}")

    def piece():
        n = at[0]
        if n >= len(pieces):
            return
        at[0] += 1
        layer, w, f, low, parts_ = pieces[n]
        flat = stg[:, n % 3, :]
        v = flat.rearrange("p (a b) -> p a b", a=4) if parts_ == 4 else flat
        d = E["pld", n]
        a = p.do("act", lambda e: e.activation(f, v, ACT.Copy), [d], inc="fh")
        b = p.do("pool", lambda e: e.tensor_tensor(v, v, f.bitcast(f32), ALU.subtract), [a], inc="fl")
        E["cnt", n] = p.do("dve", lambda e: e.tensor_scalar(
            junk, flat, 0.0, None, ALU.not_equal, ALU.add, accum_out=cnt[:, n:n + 1]),
            [b, get(("cnt", n - 1))], inc="cnt")
        src = flat.rearrange("p (a b) -> p a b", a=parts_)
        E["plo", n] = p.dma("sp", low, src, [b, E["cnt", n]], inc=f"plo{n % 3}")
        E["low", layer] = [E["plo", m] for m in range(max(0, n - 2), n + 1)]
        E["hi", layer] = a
        if n + 3 < len(pieces):
            load_piece(n + 3)
        if n + 1 == first_of[layer] + size_of[layer]:
            c = p.do("dve", lambda e: e.reduce_sum(
                tot[:, layer:layer + 1], cnt[:, first_of[layer]:n + 1], AX.X), [E["cnt", n]], inc="tot")
            E["flag", layer] = p.do("pool", lambda e: e.partition_all_reduce(
                flag[:, layer:layer + 1], tot[:, layer:layer + 1], 128, ADD), [c], inc="flag")

    junk = gg[:, :, :].rearrange("p a b -> p (a b)")

    def load_x(b):
        E["x", b] = p.dma("sp", xv[:, b % 2, :, :], x1[b], [get(("out", b - 2))], inc=f"x1{b % 2}")

    def stats(src, t, st, mv, ready, name):
        a = p.do("dve", lambda e: e.bn_stats(st[:, t, :], src), ready, inc=name + "a")
        return p.do("dve", lambda e: e.bn_aggr(mv[:, t, :], st[:, t, :]), [a], inc=name + "b")

    def norm(b):
        for t in range(NT):
            m = stats(xv[:, b % 2, t, :], t, st, mv, [E["x", b], get(("ln", b - 1))], "ln3")
        v = p.do("dve", lambda e: e.tensor_scalar_add(ve[:, :], mv[:, :, 1], EPS), [m], inc="ve3")
        r = p.do("pool", lambda e: e.tensor_tensor(rd[:, :], ve[:, :], half[:, 0:NT], ALU.pow),
                 [v, i0], inc="rd3")
        E["rd", b] = r

    def norm2(b):
        for t in range(NT):
            E["ln", b] = p.do("dve", lambda e, t=t: e.tensor_scalar(
                xn[:, t, :], xv[:, b % 2, t, :], mv[:, t, 0:1], rd[:, t:t + 1], ALU.subtract, ALU.mult),
                [E["rd", b], get(("xT", b - 1))], inc="xn3")

    def turn(b):
        for k in range(2):
            for t in range(NT):
                d = p.do("pe", lambda e, t=t, k=k: e.transpose(
                    TB[k][:, t * 128:(t + 1) * 128], xn[:, t, k * 128:(k + 1) * 128], ident[:, :]),
                    [E["ln", b], E["ident"], get(("xs", b - 1))] if t == 0 else (),
                    inc="xT3" if t == NT - 1 else None)
            w = get(("grp", b - 1, 0, KH - 1))
            a = p.do("act", lambda e, k=k: e.activation(xh[:, k, :], TB[k][:, :], ACT.Copy), [d, w], inc="xh3")
            E["xs", b] = p.do("dve", lambda e, k=k: e.tensor_tensor(
                xl[:, k, :], TB[k][:, :], xh[:, k, :].bitcast(f32), ALU.subtract), [a, w], inc="xl3")
        E["xT", b] = d

    bank = [0]
    ffree = [None] * 4

    def chain(ps, todo, after, inc):
        for n, (l, r) in enumerate(todo):
            d = p.do("pe", lambda e, l=l, r=r, n=n: e.matmul(ps, l, r, start=n == 0, stop=n == len(todo) - 1),
                     after if n == 0 else (), inc=inc if n == len(todo) - 1 else None)
        return d

    def group(b, layer, m, banks, waits, low):
        ms = slice(m * 128, (m + 1) * 128)
        src = None if layer == 0 else (b + layer - 1) % 2
        if layer == 0:
            for j, f in enumerate((f1, f2)):
                todo = []
                for k in range(2):
                    todo += [(f[:, k, ms], xh[:, k, :]), (f[:, k, ms], xl[:, k, :])]
                    if low:
                        o = (2 * j + k) * 128
                        todo.append((R[:, m % 2, o:o + 128], xh[:, k, :]))
                d = chain(FB[banks[j]][:, :], todo, waits + low if j == 0 else (), "grp")
        else:
            f = (f3, f4)[layer - 1]
            for k in range(KH):
                todo = [(f[:, k, ms], hh[src][:, k, :]), (f[:, k, ms], hl[src][:, k, :])]
                if low:
                    todo.append((R[:, m % 2, k * 128:(k + 1) * 128], hh[src][:, k, :]))
                for n, (l, r) in enumerate(todo):
                    w = [E["h", b, layer - 1, k]] if n == 0 else []
                    if n == 0 and k == 0:
                        w = w + waits + low
                    last = k == KH - 1 and n == len(todo) - 1
                    d = p.do("pe", lambda e, l=l, r=r, a=(k == 0 and n == 0), z=last: e.matmul(
                        FB[banks[0]][:, :], l, r, start=a, stop=z), w, inc="grp" if last else None)
        E["grp", b, layer, m] = d
        return d

    def layer(b, n):
        per = 2 if n == 0 else 1
        plan = []
        for m in range(KH):
            banks = [(bank[0] + j) % 4 for j in range(per)]
            bank[0] += per
            plan.append(banks)
        return plan

    def run_layer(b, n):
        plan = layer(b, n)
        saved = dict(p.value)
        chains = 2 if n == 0 else 1
        grp0, act0, dve0 = (p.value.get(s, 0) for s in ("grp", "ea", "ed"))

        def freed(m, j):
            for e_ in range(m - 1, -1, -1):
                if j in plan[e_]:
                    return free_event(e_, j)
            return ffree[j]

        def free_event(e_, j):
            if n == 0 and j == plan[e_][1]:
                return ("ed", dve0 + e_ + 1)
            return ("ea", act0 + e_ + 1)

        def waits(m):
            w = [freed(m, j) for j in plan[m]]
            if m == 0:
                w += [E["flag", n], E["hi", n]]
                if n == 0:
                    w.append(E["xs", b])
            return w

        def fast():
            for m in range(KH):
                group(b, n, m, plan[m], waits(m), [])

        fast_ops = p.capture("pe", fast)
        after_fast = dict(p.value)

        def loads():
            for m in range(KH):
                if m >= 2:
                    w = [E["grp", b, n, m - 2]]
                else:
                    w = [E["last", b, n]] + E["low", n]
                src = low12[:, m, :, :] if n == 0 else (low3, low4)[n - 1][:, m, :, :]
                size = 512 if n == 0 else 1024
                dst = R[:, m % 2, 0:size].bitcast(f32).rearrange("p (a b) -> p a b", b=128)
                E["R", m] = p.dma("sp", dst, src, w, inc=f"R{n}{m % 2}")

        sp_ops = p.capture("sp", loads)
        p.value["grp"] = grp0

        def general():
            for m in range(KH):
                group(b, n, m, plan[m], waits(m), [E["R", m]])

        general_ops = p.capture("pe", general)
        assert p.value["grp"] == after_fast["grp"]
        word = flag[0:1, n:n + 1].bitcast(i32)
        p.do("sp", None, [E["flag", n]])
        p.branch("sp", word, sp_ops)
        p.do("pe", None, [E["flag", n]])
        p.branch("pe", word, general_ops, fast_ops)
        for m in range(KH):
            for j in plan[m]:
                ffree[j] = free_event(m, j)
        E["last", b, n + 1] = E["grp", b, n, KH - 1]
        return plan

    def evacuate(b, n, m, plan):
        dst = (b + n) % 2
        u = m % 2
        g = E["grp", b, n, m]
        if n == 0:
            w = [get(("grp", b - 1, 2, KH - 1)), get(("cnt", len(pieces) - 1)) if b else None]
            a = p.do("act", lambda e: e.activation(
                gg[:, u, :], FB[plan[m][0]][:, :], ACT.Silu, scale=sc["s1"][:, m:m + 1]),
                [g, get(("gfree", u)), E["cst"], *junked()], inc="ea")
            h = p.do("dve", lambda e: e.scalar_tensor_tensor(
                out=hr[:, u, :], in0=FB[plan[m][1]][:, :], scalar=sc["s2"][:, m:m + 1], in1=gg[:, u, :],
                op0=ALU.mult, op1=ALU.mult), [g, a, get(("hfree", u))], inc="ed")
            E["gfree", u] = h
        else:
            w = []
            s_ = sc["t1" if n == 1 else "t2"]
            h = p.do("act", lambda e: e.activation(
                hr[:, u, :], FB[plan[m][0]][:, :], ACT.Gelu, scale=s_[:, m:m + 1]),
                [g, get(("hfree", u)), E["cst"]], inc="ea")
        w = [E["last", b, n]] if n else [get(("last", b - 1, 3))]
        a = p.do("dve", lambda e: e.tensor_copy(hh[dst][:, m, :], hr[:, u, :]), [h, *w], inc="hh")
        c = p.do("dve", lambda e: e.tensor_tensor(
            hl[dst][:, m, :], hr[:, u, :], hh[dst][:, m, :].bitcast(f32), ALU.subtract), [a, *w], inc="hl")
        E["hfree", u] = c
        E["h", b, n, m] = c

    def junked():
        n = at[0] - 1
        return [get(("cnt", n))]

    def last_layer(b):
        src = b % 2
        grp0 = p.value.get("w3", 0)

        def body(low):
            for t in range(NT):
                ts = slice(t * 128, (t + 1) * 128)
                ps = WB[t // 2][:, (t % 2) * 256:(t % 2) * 256 + 256]
                for k in range(KH):
                    todo = [(hh[src][:, k, ts], f5[:, k, :]), (hl[src][:, k, ts], f5[:, k, :])]
                    if low:
                        todo.append((hh[src][:, k, ts],
                                     R[:, k // 4, (k % 4) * 256:(k % 4) * 256 + 256]))
                    for n, (l, r) in enumerate(todo):
                        w = []
                        if n == 0 and t == 0:
                            w = [E["h", b, 2, k]]
                            if k == 0:
                                w += [E["flag", 3], E["hi", 3], get(("wfree", b - 1))] + low
                        z = k == KH - 1 and n == len(todo) - 1
                        d = p.do("pe", lambda e, l=l, r=r, ps=ps, a=(k == 0 and n == 0), z=z: e.matmul(
                            ps, l, r, start=a, stop=z), w, inc="w3" if z else None)
            E["last", b, 4] = d

        fast_ops = p.capture("pe", lambda: body([]))

        def loads():
            for k in range(2):
                E["R", k] = p.dma("sp", R[:, k, :].bitcast(f32).rearrange("p (a b) -> p a b", a=4),
                                  low5[:, 4 * k:4 * k + 4, :], [E["last", b, 3]] + E["low", 3], inc=f"R3{k}")

        sp_ops = p.capture("sp", loads)
        p.value["w3"] = grp0
        general_ops = p.capture("pe", lambda: body([E["R", 0], E["R", 1]]))
        word = flag[0:1, 3:4].bitcast(i32)
        p.do("sp", None, [E["flag", 3]])
        p.branch("sp", word, sp_ops)
        p.do("pe", None, [E["flag", 3]])
        p.branch("pe", word, general_ops, fast_ops)
        E["last", b + 1, 0] = E["last", b, 4]

    def finish(b):
        for t in range(NT):
            a = p.do("dve", lambda e, t=t: e.tensor_tensor(
                y[:, t, :], WB[t // 2][:, (t % 2) * 256:(t % 2) * 256 + 256], s3b[:, :], ALU.mult),
                [E["last", b, 4], E["cst"], get(("fin", b - 1))], inc="wy")
            m = stats(y[:, t, :], t, st2, mv2, [a], "ln4")
        E["wfree", b] = a
        v = p.do("dve", lambda e: e.tensor_scalar_add(ve2[:, :], mv2[:, :, 1], EPS), [m], inc="ve4")
        E["fr", b] = p.do("pool", lambda e: e.tensor_tensor(
            rd2[:, :], ve2[:, :], half[:, 0:NT], ALU.pow), [v], inc="rd4")

    def finish2(b):
        for t in range(NT):
            a = p.do("dve", lambda e, t=t: e.tensor_scalar(
                y[:, t, :], y[:, t, :], mv2[:, t, 0:1], rd2[:, t:t + 1], ALU.subtract, ALU.mult),
                [E["fr", b]], inc="yn4")
            E["fin", b] = a = p.do("dve", lambda e, t=t: e.tensor_tensor(
                xv[:, b % 2, t, :], xv[:, b % 2, t, :], y[:, t, :], ALU.add), [a], inc="x2")
        E["out", b] = p.dma("pool", out[b], xv[:, b % 2, :, :], [a], inc=f"store{b % 2}")

    load_x(0)
    for n in range(3):
        load_piece(n)
    norm(0)
    norm2(0)
    turn(0)
    for n in range(4):
        piece()
    for b in range(B):
        E.setdefault(("last", b, 0), None)
        for n in range(3):
            plan = run_layer(b, n)
            for m in range(KH):
                evacuate(b, n, m, plan)
                if b == 0:
                    piece()
                if n == 0 and m == 1 and b:
                    finish(b - 1)
                if n == 0 and m == 3 and b:
                    finish2(b - 1)
                if n == 0 and m == 4 and b + 1 < B:
                    load_x(b + 1)
                if n == 1 and m == 2 and b + 1 < B:
                    norm(b + 1)
                if n == 1 and m == 5 and b + 1 < B:
                    norm2(b + 1)
            if n == 1 and b + 1 < B:
                turn(b + 1)
        last_layer(b)
    finish(B - 1)
    finish2(B - 1)
    p.do("pool", None, [get(("out", B - 2)), E["out", B - 1]])
    p.do("sp", None, [e for e in E["low", 3]])


def kernel(**inputs):
    import concourse.bacc as bacc
    from concourse.bass_utils import run_bass_kernel_spmd as run

    def c(a):
        return np.ascontiguousarray(a)

    g = {k.replace("L0_", ""): np.asarray(v) for k, v in inputs.items()}
    wq = g["attn_w_q"].reshape(D, 4, 2, 128)
    wk = g["attn_w_kv"][:, :H * DH].reshape(D, 4, 2, 128)
    wv = g["attn_w_kv"][:, H * DH:].reshape(D, 4, 256)
    qk = np.stack([wq, wk], axis=3).reshape(D, 4, 512)
    wqkv = np.concatenate([qk, wv], axis=2).reshape(2, 128, 4, 768).transpose(1, 0, 2, 3)

    def rows(w):
        return c(w.reshape(-1, 128, w.shape[1]).transpose(1, 0, 2))

    def cols(v):
        return c(v.reshape(-1, 128).T)

    arrays = {
        "x": c(g["attn_x"].reshape(B, NT, 128, D).transpose(0, 2, 1, 3)),
        "wqkv": c(wqkv),
        "wout": rows(g["attn_w_out"]),
        "bout": c(np.broadcast_to(g["attn_b_out"], (128, D))),
        "scale": c(np.broadcast_to(g["attn_scale"].reshape(1, H), (128, H))),
        "w1": rows(g["ffn_w1_w"].T), "w2": rows(g["ffn_w2_w"].T),
        "h1": rows(g["ffn_h1_w"].T), "h2": rows(g["ffn_h2_w"].T), "w3": rows(g["ffn_w3_w"].T),
        "s1": cols(g["ffn_w1_s"]), "s2": cols(g["ffn_w2_s"]),
        "t1": cols(g["ffn_h1_s"]), "t2": cols(g["ffn_h2_s"]),
        "s3": c(np.broadcast_to(g["ffn_w3_s"], (128, D))),
    }
    nc = bacc.Bacc("TRN2", target_bir_lowering=False, num_devices=1)
    args = [nc.dram_tensor("in_" + k, a.shape, mybir.dt.from_np(a.dtype), kind="ExternalInput").ap()
            for k, a in arrays.items()]
    o = nc.dram_tensor("out_0", (B, 128, NT, D), mybir.dt.float32, kind="ExternalOutput").ap()
    build(nc, *args, o)
    r = run(nc, [{"in_" + k: a for k, a in arrays.items()}], core_ids=[0])
    got = np.asarray(r.results[0]["out_0"])
    return c(got.transpose(0, 2, 1, 3).reshape(B, S, D))
```

```python
import concourse.bass as bass
from concourse import mybir
from contextlib import ExitStack
import numpy as np

B, S, D, H, DH = 8, 512, 256, 16, 64
HP = H // 2
NT = S // 128
HID = 1024
KH = HID // 128
EPS = 1e-5
TINY = 1e-24
TOP = 80.0


class Program:

    def __init__(self):
        self.ops = {"pe": [], "act": [], "dve": [], "pool": [], "sp": []}
        self.value = {}

    def do(self, engine, fn, after=(), inc=None, by=1):
        self.ops[engine].append((fn, [e for e in after if e is not None], inc, by))
        if inc is None:
            return None
        self.value[inc] = self.value.get(inc, 0) + by
        return (inc, self.value[inc])

    def dma(self, engine, out, in_, after=(), inc=None):
        return self.do(engine, lambda e: e.dma_start(out, in_), after, inc, 16)

    def capture(self, engine, build):
        kept, self.ops[engine] = self.ops[engine], []
        build()
        taken, self.ops[engine] = self.ops[engine], kept
        return taken

    def branch(self, engine, flag, nonzero, zero=()):
        self.ops[engine].append((flag, nonzero, zero))

    def issue(self, name, engine, sems, reached):
        self.put(self.ops[name], engine, sems, reached)
        self.ops[name] = []

    def put(self, ops, engine, sems, reached):
        for op in ops:
            if len(op) == 3:
                flag, nonzero, zero = op
                word = engine.value_load(flag)
                with engine.If(word != 0):
                    self.put(nonzero, engine, sems, dict(reached))
                if zero:
                    with engine.Else():
                        self.put(zero, engine, sems, dict(reached))
                continue
            fn, after, inc, by = op
            for sem, value in after:
                if reached.get(sem, 0) < value:
                    engine.wait_ge(sems[sem], value)
                    reached[sem] = value
            if fn is None:
                continue
            done = fn(engine)
            if inc is not None:
                done.then_inc(sems[inc], by)


def run_blocks(nc, ctx, p, sems):
    for s in sorted(p.value):
        if s not in sems:
            sems[s] = ctx.enter_context(nc.semaphore("s_" + s))
    with nc.Block() as block:
        @block.sync
        def _(e):
            p.issue("sp", e, sems, {})

        @block.gpsimd
        def _(e):
            p.issue("pool", e, sems, {})

        @block.scalar
        def _(e):
            p.issue("act", e, sems, {})

        @block.vector
        def _(e):
            p.issue("dve", e, sems, {})

        @block.tensor
        def _(e):
            p.issue("pe", e, sems, {})


def attention(p, sb, banks, common, E, x, wqkv, wout, bout, scale, x1):
    f32, f32r = mybir.dt.float32, mybir.dt.float32r
    ALU, ACT, AX = mybir.AluOpType, mybir.ActivationFunctionType, mybir.AxisListType
    get = E.get
    ident, half = common["ident"], common["half"]
    wh = sb("wh", [128, 2, 4, 768], f32r)
    wl = sb("wl", [128, 2, 4, 768], f32r)
    xt = sb("xt", [128, NT, 256], f32)
    xh = sb("xh", [128, 2, 512], f32r)
    xl = sb("xl", [128, 2, 512], f32r)
    qk = sb("qk", [128, 3, NT, 256], f32)
    sq = sb("sq", [128, 512], f32)
    V = sb("V", [128, 2, NT, 512], f32r)
    th = sb("th", [128, 2, 512], f32r)
    tlq = sb("tlq", [128, 2, 512], f32r)
    tlk = sb("tlk", [128, 512], f32r)
    KS = sb("KS", [128, 3, 512], f32r)
    QS = sb("QS", [128, 3, 512], f32r)
    P = sb("P", [128, 3, 1024], f32)
    Ph = sb("Ph", [128, 3, 1024], f32r)
    Pl = sb("Pl", [128, 3, 1024], f32r)
    A = sb("A", [128, 2, 512], f32)
    AF = sb("AF", [128, 512], f32)
    ah = sb("ah", [128, 512], f32r)
    al = sb("al", [128, 512], f32r)
    ot = sb("ot", [128, 512], f32)
    rc = sb("rc", [128, 512], f32)
    rh = sb("rh", [128, 512], f32r)
    rl = sb("rl", [128, 512], f32r)
    Or = sb("Or", [128, 6, 512], f32)
    nh = sb("nh", [128, 512], f32r)
    nl = sb("nl", [128, 512], f32r)
    oh = sb("oh", [128, HP, 256], f32r)
    ol = sb("ol", [128, HP, 256], f32r)
    xr = sb("xr", [128, 2, 256], f32)
    y = sb("y", [128, 2, 256], f32)
    seld = sb("seld", [128, 240], f32r)
    selr = sb("selr", [128, 4, 128], f32r)
    bb = sb("bb", [128, 256], f32)
    es = sb("es", [128, H], f32)
    sh = sb("sh", [128, H], f32)
    eq = sb("eq", [128, 4, 2, 2, 2], f32)
    ss = sb("ss", [128, 2, 8], f32)
    rs = sb("rs", [128, 2, 8], f32)
    st, mv, ve, rd = (common[n + "3"] for n in ("st", "mv", "ve", "rd"))
    st2, mv2, ve2, rd2 = (common[n + "4"] for n in ("st", "mv", "ve", "rd"))

    SB, G, OB, DB, YB = banks[0:2], banks[2:4], banks[4], banks[5], banks[6:8]

    p.do("pool", lambda e: e.memset(ident[:, :], 0.0), inc="c0")
    p.do("pool", lambda e: e.memset(half[:, :], -0.5), inc="c0")
    p.do("pool", lambda e: e.memset(A[:, :, :], 0.0), inc="c0")
    E["c0"] = c0 = p.do("pool", lambda e: e.memset(P[:, 0, 0:240], 0.0), inc="c0")
    E["ident"] = p.do("pool", lambda e: e.affine_select(
        out=ident[:, :], in_=ident[:, :], compare_op=ALU.not_equal, fill=1.0, base=0,
        pattern=[[-1, 128]], channel_multiplier=1), [c0], inc="c1")
    c2 = p.do("pool", lambda e: e.memset(P[:, 0, 112:128], 1.0), [c0], inc="c1")
    c3 = p.do("pool", lambda e: e.affine_select(
        out=A[:, 0, :].rearrange("p (b c d) -> p b c d", b=4, c=2),
        in_=A[:, 0, :].rearrange("p (b c d) -> p b c d", b=4, c=2),
        compare_op=ALU.not_equal, fill=1.0, base=0,
        pattern=[[-32, 4], [-16, 2], [0, 64]], channel_multiplier=1), [c0], inc="c1")
    E["seld"] = p.do("dve", lambda e: e.tensor_copy(seld[:, :], P[:, 0, 0:240]), [c2], inc="c2")
    E["selr"] = p.do("dve", lambda e: e.tensor_copy(
        selr[:, :, :].rearrange("p a b -> p (a b)"), A[:, 0, :]),
        [c3], inc="c2")
    E["bb"] = p.dma("act", bb[:, :], bout, inc="bb")
    ld = p.dma("act", es[:, :], scale, inc="sc")
    E["es"] = p.do("act", lambda e: e.activation(es[:, :], es[:, :], ACT.Exp), [ld], inc="es")
    eq0 = p.do("dve", lambda e: e.memset(eq[:, :, :, :, :].rearrange("p a b c d -> p (a b c d)"), 1.0),
               inc="eq")
    for j in range(2):
        E["eq"] = p.do("dve", lambda e, j=j: e.tensor_copy(
            eq[:, :, j, 0, :], es[:, :].rearrange("p (a b d) -> p a b d", a=4, b=2)[:, :, j, :]),
            [eq0, E["es"]], inc="eq")
    sh0 = p.do("dve", lambda e: e.tensor_scalar(sh[:, :], es[:, :], -1.0, TOP, ALU.mult, ALU.add),
               [E["es"]], inc="sh")
    E["sh"] = p.do("dve", lambda e: e.tensor_scalar_min(sh[:, :], sh[:, :], 0.0), [sh0], inc="sh")

    g_at, g_free = E["g"]

    def g_take():
        i = g_at[0] % 2
        g_at[0] += 1
        return i, g_free[i]

    def split(psum, hi, lo, after, name, free=()):
        a = p.do("act", lambda e: e.activation(hi, psum, ACT.Copy), [after, *free], inc=name + "h")
        b = p.do("dve", lambda e: e.tensor_tensor(lo, psum, hi.bitcast(f32), ALU.subtract),
                 [a, *free], inc=name + "l")
        return a, b

    E["x", 0] = p.dma("sp", xt[:, :, :], x[0], inc="x")
    of = Or[:, :, :].rearrange("p a b -> p (a b)")
    stage = ([P[:, i, 0:768] for i in range(3)] + [of[:, i * 768:(i + 1) * 768] for i in range(4)]
             + [A[:, :, :].rearrange("p a b -> p (a b)")[:, 0:768]])
    wld = {}

    def load_w(n):
        wait = {0: [E["seld"]], 7: [E["selr"]]}.get(n, [])
        wld[n] = p.dma("sp", stage[n], wqkv[:, n % 2, n // 2, :], wait, inc=f"wld{n}")

    def split_w(n):
        q, k = divmod(n, 2)
        a = p.do("act", lambda e: e.activation(wh[:, k, q, :], stage[n], ACT.Copy), [wld[n]], inc="wh")
        b = p.do("dve", lambda e: e.tensor_tensor(
            wl[:, k, q, :], stage[n], wh[:, k, q, :].bitcast(f32), ALU.subtract), [a], inc="wl")
        E["w", q] = E["wlast"] = [a, b]

    ostage = [t_[:, :, :] for t_ in (y, xr)]

    def load_wo(k):
        wld["o", k] = p.dma("sp", ostage[k % 2], wout[:, 2 * k:2 * k + 2, :], get(("wo", k - 2), ()),
                            inc=f"wldo{k}")

    def split_wo(k):
        o = slice(2 * k, 2 * k + 2)
        a = p.do("act", lambda e: e.activation(oh[:, o, :], ostage[k % 2], ACT.Copy), [wld["o", k]], inc="wh")
        b = p.do("dve", lambda e: e.tensor_tensor(
            ol[:, o, :], ostage[k % 2], oh[:, o, :].bitcast(f32), ALU.subtract), [a], inc="wl")
        E["wo", k] = E["wout"] = E["wolast"] = [a, b]
        if k < 2:
            load_wo(k + 2)

    for n in range(8):
        load_w(n)
    for k in range(2):
        load_wo(k)
    for i in range(3):
        E["Pfree", i - 3] = ()

    def load_x(b):
        E["x", b] = p.dma("sp", xt[:, :, :], x[b], [get(("xT", b - 1))], inc="x")

    def stats(src, t, st, mv, ready, name):
        a = p.do("dve", lambda e: e.bn_stats(st[:, t, :], src), ready, inc=name + "a")
        return p.do("dve", lambda e: e.bn_aggr(mv[:, t, :], st[:, t, :]), [a], inc=name + "b")

    def ln1(b, t):
        m = stats(xt[:, t, :], t, st, mv, [E["x", b], get(("ln", b - 1))], "ln1")
        if t == NT - 1:
            v = p.do("dve", lambda e: e.tensor_scalar_add(ve[:, :], mv[:, :, 1], EPS), [m], inc="ve")
            E["rd", b] = p.do("pool", lambda e: e.tensor_tensor(
                rd[:, :], ve[:, :], half[:, 0:NT], ALU.pow), [v, c0], inc="rd")

    def ln1b(b, t):
        E["ln", b] = p.do("dve", lambda e: e.tensor_scalar(
            xt[:, t, :], xt[:, t, :], mv[:, t, 0:1], rd[:, t:t + 1], ALU.subtract, ALU.mult),
            [E["rd", b]], inc="xn")

    def x_turn(b, k):
        i, free = g_take()
        for t in range(NT):
            d = p.do("pe", lambda e, t=t: e.transpose(
                G[i][:, t * 128:(t + 1) * 128], xt[:, t, k * 128:(k + 1) * 128], ident[:, :]),
                [E["ln", b], E["ident"], *free] if t == 0 else (), inc="xT" if t == NT - 1 else None)
        E["xT", b] = d
        g_free[i] = split(G[i][:, :], xh[:, k, :], xl[:, k, :], d, "x", [get(("v", b - 1, 3))])
        E["xs", b] = g_free[i]

    def terms(ps, ah_, al_, bh, bl, first, last):
        todo = [(ah_, bh), (al_, bh), (ah_, bl)]
        for n_, (l, r) in enumerate(todo):
            yield (lambda e, l=l, r=r, n_=n_: e.matmul(
                ps, l, r, start=first and n_ == 0, stop=last and n_ == 2, skip_group_check=True))

    def project(b, q, t, c0_, c1_, ps, after, inc):
        fns = []
        for k in range(2):
            xs = slice(t * 128, (t + 1) * 128)
            fns += list(terms(ps, xh[:, k, xs], xl[:, k, xs], wh[:, k, q, c0_:c1_], wl[:, k, q, c0_:c1_],
                              k == 0, k == 1))
        for n_, fn in enumerate(fns):
            d = p.do("pe", fn, after if n_ == 0 else (), inc=inc if n_ == len(fns) - 1 else None)
        return d

    def qk_tile(b, q, t):
        i, free = g_take()
        d = project(b, q, t, 0, 512, G[i][:, :], [*E["xs", b], *E["w", q], *free], "qk")
        hp = b * HP + 2 * q
        u = (b * 4 + q) * NT + t
        for j in range(2):
            n_ = hp + j
            c = p.do("act", lambda e, j=j, n_=n_: e.activation(
                qk[:, n_ % 3, t, :], G[i][:, j * 256:(j + 1) * 256], ACT.Copy),
                [d, get(("T", n_ - 3))], inc="qkc")
        s = p.do("act", lambda e: e.activation(sq[:, :], G[i][:, :], ACT.Square),
                 [get(("ssum", u - 1))], inc="sq")
        g_free[i] = [s]
        m0 = p.do("dve", lambda e: e.reduce_sum(
            ss[:, u % 2, :], sq[:, :].rearrange("p (h d) -> p h d", d=DH), AX.X),
            [s, get(("rs", u - 2))], inc="ssum")
        E["ssum", u] = m0
        m1 = p.do("dve", lambda e: e.tensor_scalar_max(ss[:, u % 2, :], ss[:, u % 2, :], TINY),
                  [m0], inc="smax")
        E["rs", u] = p.do("pool", lambda e: e.tensor_tensor(
            rs[:, u % 2, :], ss[:, u % 2, :], half[:, :], ALU.pow), [m1, get(("qkn", u - 2))], inc="rs")
        return u, hp, q, t, c

    def qk_scale(u, hp, q, t, c):
        f = p.do("dve", lambda e: e.tensor_tensor(
            rs[:, u % 2, :], rs[:, u % 2, :], eq[:, q, :, :, :].rearrange("p b c d -> p (b c d)"), ALU.mult),
            [E["rs", u], E["eq"]], inc="rq")
        for j in range(2):
            a = qk[:, (hp + j) % 3, t, :].rearrange("p (h d) -> p h d", d=DH)
            r = rs[:, u % 2, 4 * j:4 * j + 4].unsqueeze(2).to_broadcast([128, 4, DH])
            E["qkn", u] = E["qkr", hp + j] = p.do(
                "dve", lambda e, a=a, r=r: e.tensor_tensor(a, a, r, ALU.mult), [f, c], inc="qkn")

    def v_tiles(b, q, half_):
        i, free = g_take()
        s = (b * 4 + q) % 2
        for t in (2 * half_, 2 * half_ + 1):
            o = (t % 2) * 256
            d = project(b, q, t, 512, 768, G[i][:, o:o + 256],
                        [*E["xs", b], *free] if t % 2 == 0 else (), "v")
        prev = b * 4 + q - 2
        w = [d, get(("pv", 4 * prev + 3))]
        moves = []
        for t in (2 * half_, 2 * half_ + 1):
            o = (t % 2) * 256
            src = G[i][:, o:o + 256].rearrange("p (a b d) -> p a b d", a=2, b=2)
            vv = V[:, s, t, :].rearrange("p (a s d) -> p a s d", a=2, s=4)
            for b_ in range(2):
                moves.append((src[:, :, b_, :], vv[:, :, 3 * b_, :], vv[:, :, 1 + b_, :]))
        for src, hi, lo in moves:
            x_ = p.do("act", lambda e, src=src, hi=hi: e.activation(hi, src, ACT.Copy), w, inc="vh")
        for src, hi, lo in moves:
            y_ = p.do("dve", lambda e, src=src, hi=hi, lo=lo: e.tensor_tensor(
                lo, src, hi.bitcast(f32), ALU.subtract), [x_, *w], inc="vl")
        g_free[i] = [x_, y_]
        E["v", b, q] = d
        E["vs", b * 4 + q] = [x_, y_]

    def turn(n_, which):
        for j in which:
            i, free = g_take()
            for t in range(NT):
                d = p.do("pe", lambda e, i=i, j=j, t=t: e.transpose(
                    G[i][:, t * 128:(t + 1) * 128], qk[:, n_ % 3, t, j * 128:(j + 1) * 128], ident[:, :]),
                    [E["qkr", n_], *free] if t == 0 else (), inc="T" if t == NT - 1 else None)
            E["T", n_] = d
            high = th[:, j, :]
            low = tlk[:, :] if j else tlq[:, n_ % 2, :]
            free = [*get(("stack", n_ - 1, j), ())]
            if j == 0:
                free.append(get(("s", 2 * (n_ - 2) + 1, NT - 1)))
            g_free[i] = hi, lo = split(G[i][:, :], high, low, d, "t", free)
            E["ts", n_] = lo
            E["made", n_, j] = hi, lo
            E["stack", n_, j] = []

    def stack(n_, j, odd):
        hi, lo = E["made", n_, j]
        g = 2 * n_ + odd
        own, other = slice(64 * odd, 64 * odd + 64), slice(64 - 64 * odd, 128 - 64 * odd)
        to = (KS if j else QS)[:, g % 3, :].bitcast(f32)
        second = (tlk[own, :], lo) if j else (th[own, j, :], hi)
        for part, (dst, (src, made)) in enumerate(((own, (th[own, j, :], hi)), (other, second))):
            E["stack", n_, j].append(p.dma(
                "sp", to[dst, :], src.bitcast(f32), [made, get(("s", g - 3, NT - 1))],
                inc=f"k{n_ % 2}{j}{odd}{part}"))

    def scores(g, jt):
        n_, r = g // 2, 64 * (g % 2)
        b_ = (NT * g + jt) % 2
        js = slice(jt * 128, (jt + 1) * 128)
        before = get(("exp", g, jt - 2)) if jt >= 2 else get(("exp", g - 1, jt + 2))
        o = 2 * (g % 2)
        ready = [*E["stack", n_, 0][o:o + 2], *E["stack", n_, 1][o:o + 2], E["ts", n_]]
        p.do("pe", lambda e: e.matmul(SB[b_][:, :], KS[:, g % 3, js], QS[:, g % 3, :],
                                      start=True, stop=False), [*ready, before])
        d = p.do("pe", lambda e: e.matmul(SB[b_][:, :], KS[r:r + 64, g % 3, js], tlq[r:r + 64, n_ % 2, :],
                                          start=False, stop=True), inc="s")
        E["s", g, jt] = d
        h = g % H
        u = 2 * g + jt // 2
        c = (jt % 2) * 512
        E["exp", g, jt] = p.do("act", lambda e: e.activation(
            P[:, u % 3, c:c + 512], SB[b_][:, :], ACT.Exp, bias=sh[:, h:h + 1]),
            [d, E["sh"], *E["Pfree", u - 3], *E["wlast"]], inc="exp")

    def parts(u):
        g, c = divmod(u, 2)
        before = get(("pvp", u - 3))
        E["ph", u] = p.do("act", lambda e: e.activation(Ph[:, u % 3, :], P[:, u % 3, :], ACT.Copy),
                          [E["exp", g, 2 * c + 1], before], inc="ph")
        E["pl", u] = p.do("dve", lambda e: e.tensor_tensor(
            Pl[:, u % 3, :], P[:, u % 3, :], Ph[:, u % 3, :].bitcast(f32), ALU.subtract),
            [E["ph", u], before], inc="pl")
        a = p.do("pool", lambda e: e.tensor_tensor(
            A[:, c, :], P[:, u % 3, 0:512], P[:, u % 3, 512:1024], ALU.add),
            [E["exp", g, 2 * c + 1], get(("fold", g - 1)), *E["wlast"]], inc="pa")
        E["Pfree", u] = [E["ph", u], E["pl", u], a]
        E["pa", u] = a

    def fold(g):
        E["fold", g] = a = p.do("pool", lambda e: e.tensor_tensor(
            AF[:, :], A[:, 0, :], A[:, 1, :], ALU.add), [E["pa", 2 * g + 1], get(("al", g - 1))], inc="pa")
        E["ah", g] = p.do("pool", lambda e: e.tensor_scalar(
            ah[:, :], AF[:, :], 1.0, 0.0, ALU.mult, ALU.add), [a, get(("den", g - 1))], inc="ah")

    def fold2(g):
        E["al", g] = p.do("dve", lambda e: e.tensor_tensor(
            al[:, :], AF[:, :], ah[:, :].bitcast(f32), ALU.subtract),
            [E["ah", g]], inc="al")

    def values(u):
        g, c = divmod(u, 2)
        q4, n_ = g // 4, g // 2
        for j in range(2):
            jt = 2 * c + j
            v = V[:, q4 % 2, jt, (g % 4) * 128:(g % 4) * 128 + 128]
            for m, src in enumerate((Ph, Pl)):
                w = ()
                if j == 0 and m == 0:
                    w = [E["ph", u], E["pl", u], *E["vs", q4], get(("oadd", g - 1))]
                d = p.do("pe", lambda e, v=v, src=src, j=j, a=(jt == 0 and m == 0),
                         z=(jt == 3 and m == 1): e.matmul(
                             OB[:, :], v, src[:, u % 3, j * 512:(j + 1) * 512], start=a, stop=z), w,
                         inc="pv" if (j == 1 and m == 1) else None)
        E["pvp", u] = E["pv", g] = d
        if c == 1:
            hi, lo = (slice(64, 128), slice(0, 64)) if g % 2 else (slice(0, 64), slice(64, 128))
            c_ = p.do("act", lambda e: e.activation(ot[hi, :], OB[lo, :], ACT.Copy),
                      [d, get(("oadd", g - 1))], inc="ot")
            E["oadd", g] = p.do("dve", lambda e: e.tensor_tensor(
                Or[hi, n_ % 6, :], OB[hi, :], ot[hi, :], ALU.add), [c_, d, get(("nl", n_ - 6)), *E["wlast"]], inc="oadd")

    def denom(g):
        h = g % 8
        s = seld[:, 112 - 16 * h:240 - 16 * h]
        w = [E["al", g], E["seld"], get(("rc", g // 8 - 1))]
        p.do("pe", lambda e: e.matmul(DB[:, :], s, ah[:, :], start=h == 0, stop=False), w)
        E["den", g] = p.do("pe", lambda e: e.matmul(DB[:, :], s, al[:, :], start=False, stop=h == 7),
                           inc="den")

    def take_sums(k):
        E["rs0", k] = p.do("act", lambda e: e.activation(rc[:, :], DB[:, :], ACT.Copy),
                           [E["den", 8 * k + 7], get(("rl", k - 1))], inc="rc0")
        E["rc", k] = E["rs0", k]

    def invert(k, j):
        cs = slice(j * 128, (j + 1) * 128)
        a = p.do("dve", lambda e: e.reciprocal(rc[:, cs], rc[:, cs]), [E["rs0", k]], inc="rc")
        if j == 3:
            w = [get(("R", 4 * k - 1))]
            b_ = p.do("dve", lambda e: e.tensor_copy(rh[:, :], rc[:, :]), [a, *w], inc="rh")
            E["rl", k] = p.do("dve", lambda e: e.tensor_tensor(
                rl[:, :], rc[:, :], rh[:, :].bitcast(f32), ALU.subtract), [b_, *w], inc="rl")

    def normal(n_):
        i, free = g_take()
        p.do("pe", lambda e: e.matmul(G[i][:, :], selr[:, n_ % 4, :], rh[:, :], start=True, stop=False),
             [E["rl", n_ // 4], E["selr"], *free])
        E["R", n_] = p.do("pe", lambda e: e.matmul(
            G[i][:, :], selr[:, n_ % 4, :], rl[:, :], start=False, stop=True), inc="R")
        o = Or[:, n_ % 6, :]
        a = p.do("dve", lambda e: e.tensor_tensor(o, G[i][:, :], o, ALU.mult),
                 [E["R", n_], E["oadd", 2 * n_ + 1]], inc="on")
        g_free[i] = [a]
        E["on", n_] = a

    def normal2(n_):
        o = Or[:, n_ % 6, :]
        a = E["on", n_]
        b_ = p.do("act", lambda e: e.activation(nh[:, :], o, ACT.Copy),
                  [a, get(("out", n_ - 1))], inc="nh")
        E["nl", n_] = p.do("dve", lambda e: e.tensor_tensor(
            nl[:, :], o, nh[:, :].bitcast(f32), ALU.subtract), [b_, get(("out", n_ - 1))], inc="nl")

    def outp(n_):
        hp = n_ % HP
        for t in range(NT):
            ts = slice(t * 128, (t + 1) * 128)
            ps = YB[t // 2][:, (t % 2) * 256:(t % 2) * 256 + 256]
            for m, (l, r) in enumerate(((nh, oh), (nl, oh), (nh, ol))):
                w = [E["nl", n_], *E["wout"], get(("yb", n_ // HP - 1))] if t == 0 and m == 0 else ()
                d = p.do("pe", lambda e, ps=ps, l=l, r=r, ts=ts, a=(hp == 0 and t % 2 == 0 and m == 0),
                         z=(hp == HP - 1 and m == 2): e.matmul(
                             ps, l[:, ts], r[:, hp, :], start=a, stop=z, skip_group_check=True), w,
                         inc="out" if (t == 3 and m == 2) else None)
        E["out", n_] = d

    def load_xr(b, half_):
        E["xr", b, half_] = p.dma("sp", xr[:, :, :], x[b][:, 2 * half_:2 * half_ + 2, :],
                                  [get("stored"), *E["wolast"]], inc="xr")

    def finish(b, t):
        a = p.do("dve", lambda e: e.tensor_tensor(
            y[:, t % 2, :], YB[t // 2][:, (t % 2) * 256:(t % 2) * 256 + 256], bb[:, :], ALU.add),
            [E["out", b * HP + HP - 1], E["bb"], get("fin"), *E["wolast"]], inc="yb")
        m = stats(y[:, t % 2, :], t, st2, mv2, [a], "ln2")
        if t % 2:
            E["yb", b] = a
            ts = slice(t - 1, t + 1)
            v = p.do("dve", lambda e: e.tensor_scalar_add(ve2[:, ts], mv2[:, ts, 1], EPS), [m], inc="ve2")
            E["fr", b, t // 2] = p.do("pool", lambda e: e.tensor_tensor(
                rd2[:, ts], ve2[:, ts], half[:, 0:2], ALU.pow), [v], inc="rd2")

    def finish2(b, t):
        a = p.do("dve", lambda e: e.tensor_scalar(
            y[:, t % 2, :], y[:, t % 2, :], mv2[:, t, 0:1], rd2[:, t:t + 1], ALU.subtract, ALU.mult),
            [E["fr", b, t // 2]], inc="yn")
        a = p.do("dve", lambda e: e.tensor_tensor(
            xr[:, t % 2, :], xr[:, t % 2, :], y[:, t % 2, :], ALU.add), [a, E["xr", b, t // 2]], inc="x1r")
        if t % 2:
            E["fin"] = E["fin", b] = a
            E["stored"] = E["x1", b] = p.dma("sp", x1[b][:, t - 1:t + 1, :], xr[:, :, :], [a], inc="x1")
            if t == 1:
                load_xr(b, 1)

    yield
    NU = 2 * B * H
    pend, qscale, norms = {}, {}, {}

    def later(i, fn, *args):
        pend.setdefault(i, []).append((fn, args))

    for t in range(NT):
        ln1(0, t)
    for t in range(NT):
        ln1b(0, t)
    x_turn(0, 0)
    x_turn(0, 1)
    split_w(0)
    split_w(1)
    prev = None
    for t in range(NT):
        u = qk_tile(0, 0, t)
        if prev:
            qk_scale(*prev)
        prev = u
    v_tiles(0, 0, 0)
    qk_scale(*prev)
    split_w(2)
    turn(0, (0, 1))
    for j in (0, 1):
        for odd in (0, 1):
            stack(0, j, odd)
    split_w(3)
    v_tiles(0, 0, 1)
    split_w(7)

    for i in range(NU + 13):
        g, c = divmod(i, 2)
        live = i < NU
        b, h = divmod(g, H)
        r = i % 8
        nb, nq = (b, h // 4 + 1) if h < 12 else (b + 1, 0)
        more = live and nb < B
        i16, k8 = i % 16, i // 16 - 1
        tail = i - NU if i >= NU else -1
        if live:
            scores(g, 2 * c)
            scores(g, 2 * c + 1)
        if 0 <= i - 3 < NU:
            values(i - 3)
        if i < 3:
            split_w(4 + i)
        if i in (5, 6, 12, 13):
            split_wo(i - 5 if i < 7 else i - 10)
        if 0 <= i - 1 < NU:
            parts(i - 1)
        if more and r < 4:
            qscale[i + 1] = qk_tile(nb, nq, r)
        if i16 in (11, 13, 15) and 0 <= k8 < 2 * B - 1:
            outp(4 * k8 + (i16 - 11) // 2)
        if i16 == 1 and 1 <= k8 <= 2 * B - 1:
            outp(4 * k8 - 1)
        if 7 <= tail <= 10:
            outp(4 * (2 * B - 1) + tail - 7)
        if i in norms:
            normal2(norms.pop(i))
        if more and r in (5, 6):
            turn(i // 4 + 1, (6 - r,))
            stack(i // 4 + 1, 6 - r, 0)
            later(i + 1, stack, i // 4 + 1, 6 - r, 1)
        for fn, args in pend.pop(i, []):
            fn(*args)
        if i in qscale:
            qk_scale(*qscale.pop(i))
        if more and (r == 4 or r == (5 if nq == 3 else 7)):
            v_tiles(nb, nq, r // 5)
        n_ = None
        if i16 in (9, 10, 12, 14) and 0 <= k8 < 2 * B - 1:
            n_ = 4 * k8 + (i16 - 8) // 2
        if 5 <= tail <= 8:
            n_ = 4 * (2 * B - 1) + tail - 5
        if n_ is not None:
            normal(n_)
            norms[i + 1] = n_
        if c == 0 and 0 <= g - 2 < B * H:
            denom(g - 2)
        if c == 1 and 0 <= g - 1 < B * H:
            fold2(g - 1)
        if c == 0 and 0 <= g - 1 < B * H:
            fold(g - 1)
        if live and r in (0, 1):
            turn(i // 4 + 1, (1 - r,))
            stack(i // 4 + 1, 1 - r, 0)
            later(i + 1, stack, i // 4 + 1, 1 - r, 1)
        if tail == 4:
            for j in range(4):
                invert(k8, j)
        elif 0 <= k8 < 2 * B - 1 and i16 in (4, 5, 6, 7):
            invert(k8, i16 - 4)
        if 0 <= k8 < 2 * B and i16 == 3:
            take_sums(k8)
        i32, pb_ = i % 32, i // 32 - 1
        if tail == 11:
            for t, fn in enumerate((finish, finish, finish2, finish2)):
                fn(B - 1, t % 2)
            for t in (2, 3):
                finish(B - 1, t)
        if tail == 12:
            for t in (2, 3):
                finish2(B - 1, t)
        if 0 <= pb_ < B - 1:
            if i32 in (17, 18, 21, 22):
                finish(pb_, (i32 - 17) // 4 * 2 + (i32 - 17) % 2)
            if i32 in (19, 20, 23, 24):
                finish2(pb_, (i32 - 19) // 4 * 2 + (i32 - 19) % 2)
        if b + 1 < B:
            if i32 == 0:
                load_x(b + 1)
            if i32 in (8, 9, 10, 11):
                ln1(b + 1, i32 - 8)
            if i32 in (13, 14, 15, 16):
                ln1b(b + 1, i32 - 13)
            if i32 == 22:
                x_turn(b + 1, 0)
            if i32 == 23:
                x_turn(b + 1, 1)
        if live and i32 == 28:
            load_xr(b, 0)
        if i == NU - 7:
            E["w1"] = [E["v", B - 1, 3], E["T", B * HP - 1], E["qkr", B * HP - 1], E["ln", B - 1]]
        if i == NU + 2:
            u = NU - 1
            E["w2"] = [E["pv", B * H - 1], E["ph", u], E["pl", u], E["den", B * H - 1]]
            E["banks"] = [E["exp", B * H - 1, NT - 1], E["exp", B * H - 1, NT - 1], E["oadd", B * H - 1], None]
        if tail == 4:
            E["banks"][3] = E["rs0", k8]
        if tail == 10:
            E["w3"] = [E["out", B * HP - 1], E["nl", B * HP - 1]]
        if tail == 12:
            E["w4"] = [E["x1", B - 1], E["fin", B - 1]]
            E["yb"] = [E["yb", B - 1]]
        yield i


def build(nc, x, wqkv, wout, bout, scale, w1, w2, h1, h2, w3, s1, s2, t1, t2, s3, out):
    f32 = mybir.dt.float32
    x1 = nc.dram_tensor("x1", (B, 128, NT, 256), f32, kind="Internal").ap()
    lows = [nc.dram_tensor("low%d" % i, s, f32, kind="Internal").ap() for i, s in enumerate((
        (128, KH, 4, 128), (128, KH, KH, 128), (128, KH, KH, 128), (128, KH, D)))]
    with ExitStack() as ctx:
        p = Program()
        E = {"g": ([0], [[], []])}

        def on(stack):
            return lambda name, shape, dt: stack.enter_context(nc.sbuf_tensor(name, shape, dt))

        banks = [ctx.enter_context(nc.psum_tensor(f"bank{i}", [128, 512], f32)) for i in range(8)]
        sb = on(ctx)
        common = {
            "ident": sb("ident", [128, 128], f32), "half": sb("half", [128, 8], f32),
            "cnt": sb("cnt", [128, 32], f32), "tot": sb("tot", [128, 4], f32),
            "flag": sb("flag", [128, 4], f32), "pre": sb("pre", [128, 1], f32),
        }
        for n in ("s1", "s2", "t1", "t2"):
            common[n] = sb("c" + n, [128, KH], f32)
        for n in ("3", "4"):
            for m, shape in (("st", [128, NT, 6]), ("mv", [128, NT, 2]), ("ve", [128, NT]), ("rd", [128, NT])):
                common[m + n] = sb(m + n, shape, f32)
        with ExitStack() as a:
            first = attention(p, on(a), banks, common, E, x, wqkv, wout, bout, scale, x1)
            next(first)
        with ExitStack() as a:
            second = feed_forward(p, on(a), banks, common, E, x1, lows, w1, w2, h1, h2, w3,
                                  s1, s2, t1, t2, s3, out)
            next(second)
        n = 2 * B * H
        for i in first:
            if i >= n - 7:
                next(second)
        for _ in second:
            pass
        run_blocks(nc, ctx, p, {})


def feed_forward(p, sb, banks, common, EA, x1, lows, w1, w2, h1, h2, w3, s1, s2, t1, t2, s3, out):
    f32, f32r, i32 = mybir.dt.float32, mybir.dt.float32r, mybir.dt.int32
    ALU, ACT, AX = mybir.AluOpType, mybir.ActivationFunctionType, mybir.AxisListType
    E = {}
    get = E.get
    ADD = bass.bass_isa.ReduceOp.add

    ident, half, cnt, tot, flag = (common[n] for n in ("ident", "half", "cnt", "tot", "flag"))
    sc = {n: common[n] for n in ("s1", "s2", "t1", "t2")}
    pre = common["pre"]
    st, mv, ve, rd = (common[n + "3"] for n in ("st", "mv", "ve", "rd"))
    st2, mv2, ve2, rd2 = (common[n + "4"] for n in ("st", "mv", "ve", "rd"))
    f1 = sb("f1", [128, 2, HID], f32r)
    f2 = sb("f2", [128, 2, HID], f32r)
    f3 = sb("f3", [128, KH, HID], f32r)
    stg = sb("stg", [128, 3, 1024], f32)
    xv = sb("xv", [128, 2, NT, D], f32)
    xn = sb("xn", [128, NT, D], f32)
    junk = sb("junk", [128, 1024], mybir.dt.uint8)
    xh = sb("xh2", [128, 2, 512], f32r)
    xl = sb("xl2", [128, 2, 512], f32r)
    gg = sb("gg", [128, 2, 512], f32)
    hr = sb("hr", [128, 2, 512], f32)
    hh0 = sb("hh0", [128, KH, 512], f32r)
    hl0 = sb("hl0", [128, KH, 512], f32r)
    R = sb("R", [128, 2, 1024], f32r)
    f4 = sb("f4", [128, KH, HID], f32r)
    hh1 = sb("hh1", [128, KH, 512], f32r)
    hl1 = sb("hl1", [128, KH, 512], f32r)
    f5 = sb("f5", [128, KH, D], f32r)
    y = sb("yf", [128, NT, D], f32)
    s3b = sb("s3b", [128, D], f32)
    hh, hl = (hh0, hh1), (hl0, hl1)

    FB, TB, WB = [banks[0], banks[1], banks[4], banks[5]], banks[2:4], banks[6:8]
    yield
    for n, src in (("s1", s1), ("s2", s2), ("t1", t1), ("t2", t2)):
        E["cst"] = p.dma("sp", sc[n][:, :], src, inc="cst")
    i0 = EA["c0"]
    E["ident"] = EA["ident"]

    low12, low3, low4, low5 = lows
    pieces = []
    for j, (w, f) in enumerate(((w1, f1), (w2, f2))):
        for k in range(2):
            pieces.append((0, w[:, k, :], f[:, k, :], low12[:, :, 2 * j + k, :], 8))
    for n, (w, f, low) in enumerate(((h1, f3, low3), (h2, f4, low4))):
        for k in range(KH):
            pieces.append((1 + n, w[:, k, :], f[:, k, :], low[:, :, k, :], 8))
    for k in range(2):
        pieces.append((3, w3[:, 4 * k:4 * k + 4, :], f5[:, 4 * k:4 * k + 4, :], low5[:, 4 * k:4 * k + 4, :], 4))
    at = [0]
    first_of = {0: 0, 1: 4, 2: 12, 3: 20}
    size_of = {0: 4, 1: 8, 2: 8, 3: 2}

    def load_piece(n):
        layer, w, f, low, parts_ = pieces[n]
        v = stg[:, n % 3, :]
        if parts_ == 4:
            v = v.rearrange("p (a b) -> p a b", a=4)
        E["pld", n] = p.dma("sp", v, w, [get(("plo", n - 3)), *(EA["w1"] if n < 3 else ())],
                            inc=f"pld{n % 3}")


    def freed(n):
        return "w1" if n < 12 else "w2" if n < 19 else "w3" if n < 20 else "w4"

    def split_piece():
        n = at[0]
        if n < len(pieces):
            layer, w, f, low, parts_ = pieces[n]
            flat = stg[:, n % 3, :]
            v = flat.rearrange("p (a b) -> p a b", a=4) if parts_ == 4 else flat
            a = p.do("act", lambda e: e.activation(f, v, ACT.Copy), [E["pld", n], *EA[freed(n)]], inc="fh")
            E["split", n] = p.do("pool", lambda e: e.tensor_tensor(v, v, f.bitcast(f32), ALU.subtract),
                                 [a], inc="fl")
            E["hi", layer] = a
        at[0] += 1

    def count_piece():
        n = at[0] - 1
        if not 0 <= n < len(pieces):
            return
        layer, w, f, low, parts_ = pieces[n]
        flat = stg[:, n % 3, :]
        b = E["split", n]
        E["cnt", n] = p.do("dve", lambda e: e.tensor_scalar(
            junk[:, :], flat, 0.0, None, ALU.not_equal, ALU.add, accum_out=cnt[:, n:n + 1]),
            [b, get(("cnt", n - 1)), *EA["w1"]], inc="cnt")
        src = flat.rearrange("p (a b) -> p a b", a=parts_)
        E["plo", n] = p.dma("sp", low, src, [b, E["cnt", n]], inc=f"plo{n % 3}")
        E["low", layer] = [E["plo", m] for m in range(max(0, n - 2), n + 1)]
        if n + 3 < len(pieces):
            load_piece(n + 3)
        if n + 1 == first_of[layer] + size_of[layer]:
            c = p.do("dve", lambda e: e.reduce_sum(
                tot[:, layer:layer + 1], cnt[:, first_of[layer]:n + 1], AX.X), [E["cnt", n]], inc="tot")
            E["flag", layer] = p.do("pool", lambda e: e.partition_all_reduce(
                flag[:, layer:layer + 1], tot[:, layer:layer + 1], 128, ADD), [c], inc="flag")

    def piece():
        count_piece()
        split_piece()

    def load_x(b):
        E["x", b] = p.dma("sp", xv[:, b % 2, :, :], x1[b],
                          [get(("out", b - 2)), EA["x1", b], *EA["w1"]], inc=f"x1{b % 2}")

    def stats(src, t, st, mv, ready, name):
        a = p.do("dve", lambda e: e.bn_stats(st[:, t, :], src), ready, inc=name + "a")
        return p.do("dve", lambda e: e.bn_aggr(mv[:, t, :], st[:, t, :]), [a], inc=name + "b")

    def norm(b, t):
        m = stats(xv[:, b % 2, t, :], t, st, mv, [E["x", b], get(("ln", b - 1))], "ln3")
        if t == NT - 1:
            v = p.do("dve", lambda e: e.tensor_scalar_add(ve[:, :], mv[:, :, 1], EPS), [m], inc="ve3")
            E["rd", b] = p.do("pool", lambda e: e.tensor_tensor(
                rd[:, :], ve[:, :], half[:, 0:NT], ALU.pow), [v, i0], inc="rd3")

    def norm2(b, t):
        E["ln", b] = p.do("dve", lambda e: e.tensor_scalar(
            xn[:, t, :], xv[:, b % 2, t, :], mv[:, t, 0:1], rd[:, t:t + 1], ALU.subtract, ALU.mult),
            [E["rd", b], get(("xT", b - 1)), *EA["w1"]], inc="xn3")

    def turn(b):
        g_at, g_free = EA["g"]
        for k in range(2):
            i = g_at[0] % 2
            g_at[0] += 1
            for t in range(NT):
                d = p.do("pe", lambda e, t=t, k=k, i=i: e.transpose(
                    TB[i][:, t * 128:(t + 1) * 128], xn[:, t, k * 128:(k + 1) * 128], ident[:, :]),
                    [E["ln", b], E["ident"], *g_free[i]] if t == 0 else (),
                    inc="xT3" if t == NT - 1 else None)
            w = [get(("grp", b - 1, 0, KH - 1)), *EA["w2"]]
            a = p.do("act", lambda e, k=k, i=i: e.activation(xh[:, k, :], TB[i][:, :], ACT.Copy),
                     [d, *w], inc="xh3")
            c = p.do("dve", lambda e, k=k, i=i: e.tensor_tensor(
                xl[:, k, :], TB[i][:, :], xh[:, k, :].bitcast(f32), ALU.subtract), [a, *w], inc="xl3")
            E["xs", b] = c
            g_free[i] = [a, c]
        E["xT", b] = d

    bank = [0]
    ffree = []

    def chain(ps, todo, after, inc):
        for n, (l, r) in enumerate(todo):
            d = p.do("pe", lambda e, l=l, r=r, n=n: e.matmul(ps, l, r, start=n == 0, stop=n == len(todo) - 1),
                     after if n == 0 else (), inc=inc if n == len(todo) - 1 else None)
        return d

    def group(b, layer, m, banks, waits, low):
        ms = slice(m * 128, (m + 1) * 128)
        src = None if layer == 0 else (b + layer - 1) % 2
        if layer == 0:
            for j, f in enumerate((f1, f2)):
                todo = []
                for k in range(2):
                    todo += [(f[:, k, ms], xh[:, k, :]), (f[:, k, ms], xl[:, k, :])]
                    if low:
                        o = (2 * j + k) * 128
                        todo.append((R[:, m % 2, o:o + 128], xh[:, k, :]))
                d = chain(FB[banks[j]][:, :], todo, waits + low if j == 0 else (), "grp")
        else:
            f = (f3, f4)[layer - 1]
            for k in range(KH):
                todo = [(f[:, k, ms], hh[src][:, k, :]), (f[:, k, ms], hl[src][:, k, :])]
                if low:
                    todo.append((R[:, m % 2, k * 128:(k + 1) * 128], hh[src][:, k, :]))
                for n, (l, r) in enumerate(todo):
                    w = [E["h", b, layer - 1, k]] if n == 0 else []
                    if n == 0 and k == 0:
                        w = w + waits + low
                    last = k == KH - 1 and n == len(todo) - 1
                    d = p.do("pe", lambda e, l=l, r=r, a=(k == 0 and n == 0), z=last: e.matmul(
                        FB[banks[0]][:, :], l, r, start=a, stop=z), w, inc="grp" if last else None)
        E["grp", b, layer, m] = d
        return d

    def run_groups(b, n, ms):
        per = 2 if n == 0 else 1
        if not ffree:
            ffree.extend(EA["banks"])
        plan = {}
        waits = {}
        act0, dve0 = (p.value.get(s, 0) for s in ("ea", "ed"))
        for at_, m in enumerate(ms):
            plan[m] = [(bank[0] + j) % 4 for j in range(per)]
            bank[0] += per
            waits[m] = [ffree[j] for j in plan[m]]
            if m == 0:
                waits[m] += [E["flag", n], E["hi", n]]
                if n == 0:
                    waits[m].append(E["xs", b])
            ffree[plan[m][0]] = ("ea", act0 + at_ + 1)
            if n == 0:
                ffree[plan[m][1]] = ("ed", dve0 + at_ + 1)
        grp0 = p.value.get("grp", 0)

        def fast():
            for m in ms:
                group(b, n, m, plan[m], waits[m], [])

        fast_ops = p.capture("pe", fast)
        after_fast = p.value["grp"]

        def loads():
            for m in ms:
                if m >= 2:
                    w = [E["grp", b, n, m - 2]]
                else:
                    w = [E["last", b, n]] + E["low", n] + EA["w2"]
                src = low12[:, m, :, :] if n == 0 else (low3, low4)[n - 1][:, m, :, :]
                size = 512 if n == 0 else 1024
                dst = R[:, m % 2, 0:size].bitcast(f32).rearrange("p (a b) -> p a b", b=128)
                E["R", m] = p.dma("sp", dst, src, w, inc=f"R{n}{m % 2}")

        sp_ops = p.capture("sp", loads)
        p.value["grp"] = grp0

        def general():
            for m in ms:
                group(b, n, m, plan[m], waits[m], [E["R", m]])

        general_ops = p.capture("pe", general)
        assert p.value["grp"] == after_fast
        word = flag[0:1, n:n + 1].bitcast(i32)
        p.do("sp", None, [E["flag", n]])
        p.branch("sp", word, sp_ops)
        p.do("pe", None, [E["flag", n]])
        p.branch("pe", word, general_ops, fast_ops)
        E["last", b, n + 1] = E["grp", b, n, ms[-1]]
        return plan

    def evacuate(b, n, m, plan):
        u = m % 2
        g = E["grp", b, n, m]
        if n == 0:
            a = p.do("act", lambda e: e.activation(
                gg[:, u, :], FB[plan[m][0]][:, :], ACT.Silu, scale=sc["s1"][:, m:m + 1]),
                [g, get(("gfree", u)), E["cst"], *EA["w2"]], inc="ea")
            h = p.do("dve", lambda e: e.scalar_tensor_tensor(
                out=hr[:, u, :], in0=FB[plan[m][1]][:, :], scalar=sc["s2"][:, m:m + 1], in1=gg[:, u, :],
                op0=ALU.mult, op1=ALU.mult), [g, a, get(("hfree", u))], inc="ed")
            E["gfree", u] = h
            E["raw", b, n, m] = h
        else:
            s_ = sc["t1" if n == 1 else "t2"]
            h = p.do("act", lambda e: e.activation(
                hr[:, u, :], FB[plan[m][0]][:, :], ACT.Gelu, scale=s_[:, m:m + 1]),
                [g, get(("hfree", u)), E["cst"]], inc="ea")
            E["raw", b, n, m] = h

    def halves(b, n, m):
        dst = (b + n) % 2
        u = m % 2
        h = E["raw", b, n, m]
        w = [E["last", b, n] if n else get(("last", b - 1, 4)), *EA["w3" if dst else "w2"]]
        hi, lo, raw = hh[dst][:, m, :], hl[dst][:, m, :], hr[:, u, :]
        if n == 0:
            a = p.do("act", lambda e: e.activation(hi, raw, ACT.Copy), [h, *w], inc="hh0")
        else:
            a = p.do("dve", lambda e: e.tensor_copy(hi, raw), [h, *w], inc="hh")
        c = p.do("dve", lambda e: e.tensor_tensor(lo, raw, hi.bitcast(f32), ALU.subtract), [a, *w], inc="hl")
        E["hfree", u] = c
        E["h", b, n, m] = c

    def last_layer(b):
        src = b % 2
        grp0 = p.value.get("w3", 0)

        def body(low):
            for t in range(NT):
                ts = slice(t * 128, (t + 1) * 128)
                ps = WB[t // 2][:, (t % 2) * 256:(t % 2) * 256 + 256]
                for k in range(KH):
                    todo = [(hh[src][:, k, ts], f5[:, k, :]), (hl[src][:, k, ts], f5[:, k, :])]
                    if low:
                        todo.append((hh[src][:, k, ts],
                                     R[:, k // 4, (k % 4) * 256:(k % 4) * 256 + 256]))
                    for n, (l, r) in enumerate(todo):
                        w = []
                        if n == 0 and t == 0:
                            w = [E["h", b, 2, k]]
                            if k == 0:
                                w += [E["flag", 3], E["hi", 3], *EA["yb"], get(("wfree", b - 1))] + low
                        z = k == KH - 1 and n == len(todo) - 1
                        d = p.do("pe", lambda e, l=l, r=r, ps=ps, a=(k == 0 and n == 0), z=z: e.matmul(
                            ps, l, r, start=a, stop=z), w, inc="w3" if z else None)
            E["last", b, 4] = d

        fast_ops = p.capture("pe", lambda: body([]))

        def loads():
            for k in range(2):
                E["R", k] = p.dma("sp", R[:, k, :].bitcast(f32).rearrange("p (a b) -> p a b", a=4),
                                  low5[:, 4 * k:4 * k + 4, :], [E["last", b, 3]] + E["low", 3], inc=f"R3{k}")

        sp_ops = p.capture("sp", loads)
        p.value["w3"] = grp0
        general_ops = p.capture("pe", lambda: body([E["R", 0], E["R", 1]]))
        word = flag[0:1, 3:4].bitcast(i32)
        p.do("sp", None, [E["flag", 3]])
        p.branch("sp", word, sp_ops)
        p.do("pe", None, [E["flag", 3]])
        p.branch("pe", word, general_ops, fast_ops)
        E["last", b + 1, 0] = E["last", b, 4]

    def finish(b, t):
        a = p.do("dve", lambda e: e.tensor_tensor(
            y[:, t, :], WB[t // 2][:, (t % 2) * 256:(t % 2) * 256 + 256], s3b[:, :], ALU.mult),
            [E["last", b, 4], E["s3"], get(("fin", b - 1)), *EA["w4"]], inc="wy")
        m = stats(y[:, t, :], t, st2, mv2, [a], "ln4")
        if t == NT - 1:
            E["wfree", b] = a
            v = p.do("dve", lambda e: e.tensor_scalar_add(ve2[:, :], mv2[:, :, 1], EPS), [m], inc="ve4")
            E["fr", b] = p.do("pool", lambda e: e.tensor_tensor(
                rd2[:, :], ve2[:, :], half[:, 0:NT], ALU.pow), [v], inc="rd4")

    def finish2(b, t):
        a = p.do("dve", lambda e: e.tensor_scalar(
            y[:, t, :], y[:, t, :], mv2[:, t, 0:1], rd2[:, t:t + 1], ALU.subtract, ALU.mult),
            [E["fr", b]], inc="yn4")
        E["fin", b] = a = p.do("dve", lambda e: e.tensor_tensor(
            xv[:, b % 2, t, :], xv[:, b % 2, t, :], y[:, t, :], ALU.add), [a], inc="x2")
        if t == NT - 1:
            E["out", b] = p.dma("pool", out[b], xv[:, b % 2, :, :], [a], inc=f"store{b % 2}")

    load_x(0)
    for n in range(3):
        load_piece(n)
    yield
    for n in range(10):
        if n >= 2:
            piece()
        if n in (1, 2):
            norm(0, 2 * n - 2)
            norm(0, 2 * n - 1)
        if n in (4, 5):
            norm2(0, 2 * n - 8)
            norm2(0, 2 * n - 7)
        if n == 8:
            turn(0)
            plan = {}
        yield
    E["last", 0, 0] = None
    for ms in ((0, 1), (2,), (3,), (4,), (5,), (6,), (7,)):
        plan = run_groups(0, 0, ms)
        for m in ms:
            evacuate(0, 0, m, plan)
            halves(0, 0, m)
        if at[0] < 19:
            piece()
        yield
    yield
    yield
    E["s3"] = p.dma("sp", s3b[:, :], s3, EA["w4"], inc="s3")
    for b in range(B):
        for n in range(3):
            if n == 0 and b == 0:
                continue
            plan = run_groups(b, n, range(KH))
            for m in range(KH):
                if n == 0 and m == KH - 1:
                    halves(b, n, m - 1)
                evacuate(b, n, m, plan)
                if n or m == KH - 1:
                    halves(b, n, m)
                elif m:
                    halves(b, n, m - 1)
                if b == 0:
                    piece()
                if n == 1 and b:
                    finish(b - 1, m) if m < NT else finish2(b - 1, m - NT)
                if n == 1 and m == KH - 1 and b + 1 < B:
                    load_x(b + 1)
                if n == 2 and b + 1 < B:
                    if m in (1, 2):
                        norm(b + 1, 2 * m - 2)
                        norm(b + 1, 2 * m - 1)
                    if m in (4, 5):
                        norm2(b + 1, 2 * m - 8)
                        norm2(b + 1, 2 * m - 7)
        if b + 1 < B:
            turn(b + 1)
            E["pre"] = p.do("act", lambda e: e.activation(pre[:, :], sc["s1"][:, 0:1], ACT.Silu),
                            [E["cst"], get("pre")], inc="pre")
        last_layer(b)
    for t in range(NT):
        finish(B - 1, t)
    for t in range(NT):
        finish2(B - 1, t)
    p.do("pool", None, [get(("out", B - 2)), E["out", B - 1]])
    p.do("sp", None, E["low", 3])
    yield


def kernel(**inputs):
    import concourse.bacc as bacc
    from concourse.bass_utils import run_bass_kernel_spmd as run

    def c(a):
        return np.ascontiguousarray(a)

    g = {k.replace("L0_", ""): np.asarray(v) for k, v in inputs.items()}
    wq = g["attn_w_q"].reshape(D, 4, 2, 128)
    wk = g["attn_w_kv"][:, :H * DH].reshape(D, 4, 2, 128)
    wv = g["attn_w_kv"][:, H * DH:].reshape(D, 4, 256)
    qk = np.stack([wq, wk], axis=3).reshape(D, 4, 512)
    wqkv = np.concatenate([qk, wv], axis=2).reshape(2, 128, 4, 768).transpose(1, 0, 2, 3)

    def rows(w):
        return c(w.reshape(-1, 128, w.shape[1]).transpose(1, 0, 2))

    def cols(v):
        return c(v.reshape(-1, 128).T)

    arrays = {
        "x": c(g["attn_x"].reshape(B, NT, 128, D).transpose(0, 2, 1, 3)),
        "wqkv": c(wqkv),
        "wout": rows(g["attn_w_out"]),
        "bout": c(np.broadcast_to(g["attn_b_out"], (128, D))),
        "scale": c(np.broadcast_to(g["attn_scale"].reshape(1, H), (128, H))),
        "w1": rows(g["ffn_w1_w"].T), "w2": rows(g["ffn_w2_w"].T),
        "h1": rows(g["ffn_h1_w"].T), "h2": rows(g["ffn_h2_w"].T), "w3": rows(g["ffn_w3_w"].T),
        "s1": cols(g["ffn_w1_s"]), "s2": cols(g["ffn_w2_s"]),
        "t1": cols(g["ffn_h1_s"]), "t2": cols(g["ffn_h2_s"]),
        "s3": c(np.broadcast_to(g["ffn_w3_s"], (128, D))),
    }
    nc = bacc.Bacc("TRN2", target_bir_lowering=False, num_devices=1)
    args = [nc.dram_tensor("in_" + k, a.shape, mybir.dt.from_np(a.dtype), kind="ExternalInput").ap()
            for k, a in arrays.items()]
    o = nc.dram_tensor("out_0", (B, 128, NT, D), mybir.dt.float32, kind="ExternalOutput").ap()
    build(nc, *args, o)
    r = run(nc, [{"in_" + k: a for k, a in arrays.items()}], core_ids=[0])
    got = np.asarray(r.results[0]["out_0"])
    return c(got.transpose(0, 2, 1, 3).reshape(B, S, D))
```
